# Optimizing a Trainium2 kernel written in Bass

```python
import numpy as np
import jax
import jax.numpy as jnp

def _softmax(x, axis=-1):
    return jax.nn.softmax(x, axis=axis)

def _gelu(x):
    return jax.nn.gelu(x, approximate=True)

def _silu(x):
    return jax.nn.silu(x)

def _sigmoid(x):
    return jax.nn.sigmoid(x)

def _layernorm(x, axis=-1, eps=1e-05):
    m = jnp.mean(x, axis=axis, keepdims=True)
    v = jnp.var(x, axis=axis, keepdims=True)
    return (x - m) / jnp.sqrt(v + eps)

def _scatter_add(tgt, idx, src, axis=0):
    return tgt.at[idx].add(src)

def _segment_sum(src, seg, n):
    return jax.ops.segment_sum(src, seg, n)
kernel_name = 'mk_seq_postln_d1_jaxref_r4_94fb8f'

def setup_inputs(seed: int=0):
    np.random.seed(seed)
    _w = jnp.asarray

    def _L0_attn_setup():
        import math
        import jax, jax.numpy as jnp
        import numpy as np
        N_EMBD = 256
        N_HEAD = 16
        NUM_BUCKETS = 32
        MAX_DISTANCE = 128

        def _relative_position_bucket(relative_position, num_buckets=NUM_BUCKETS, max_distance=MAX_DISTANCE):
            rp = -jnp.minimum(relative_position, 0)
            max_exact = num_buckets // 2
            is_small = rp < max_exact
            rp_large = max_exact + (jnp.log(rp.astype(jnp.float32) / max_exact + 1e-10) / math.log(max_distance / max_exact) * (num_buckets - max_exact)).astype(jnp.int32)
            rp_large = jnp.minimum(rp_large, num_buckets - 1)
            return jnp.where(is_small, rp, rp_large)
        key = jax.random.key(seed)
        ks = jax.random.split(key, 6)
        B, T, C = (4, 512, N_EMBD)
        s_in = 1.0 / math.sqrt(C)
        x = jax.random.normal(ks[0], (B, T, C), dtype=jnp.float32)
        W_attn = jax.random.normal(ks[1], (3 * C, C), dtype=jnp.float32) * s_in
        b_attn = jnp.zeros((3 * C,), dtype=jnp.float32)
        W_proj = jax.random.normal(ks[2], (C, C), dtype=jnp.float32) * s_in
        b_proj = jnp.zeros((C,), dtype=jnp.float32)
        rel_emb = jax.random.normal(ks[3], (NUM_BUCKETS, N_HEAD), dtype=jnp.float32) * 0.02
        return {'x': x, 'W_attn': W_attn, 'b_attn': b_attn, 'W_proj': W_proj, 'b_proj': b_proj, 'rel_emb': rel_emb}
    _L0_attn_in = _L0_attn_setup()

    def _L0_ffn_setup():
        import jax, jax.numpy as jnp
        import numpy as np
        D_MODEL = 256
        HIDDEN = 1024
        N_ROUTING = 2
        key = jax.random.key(seed)
        ks = jax.random.split(key, 10)
        s = 0.02
        x = jax.random.normal(ks[0], (4, 1024, D_MODEL), dtype=jnp.float32)
        gate_w = jax.random.normal(ks[1], (N_ROUTING, D_MODEL), dtype=jnp.float32) * s
        w1 = jax.random.normal(ks[2], (N_ROUTING, D_MODEL, HIDDEN), dtype=jnp.float32) * s
        b1 = jax.random.normal(ks[3], (N_ROUTING, HIDDEN), dtype=jnp.float32) * s
        w2 = jax.random.normal(ks[4], (N_ROUTING, HIDDEN, D_MODEL), dtype=jnp.float32) * s
        b2 = jax.random.normal(ks[5], (N_ROUTING, D_MODEL), dtype=jnp.float32) * s
        sw1 = jax.random.normal(ks[6], (D_MODEL, HIDDEN), dtype=jnp.float32) * s
        sb1 = jax.random.normal(ks[7], (HIDDEN,), dtype=jnp.float32) * s
        sw2 = jax.random.normal(ks[8], (HIDDEN, D_MODEL), dtype=jnp.float32) * s
        sb2 = jax.random.normal(ks[9], (D_MODEL,), dtype=jnp.float32) * s
        return {'x': x, 'gate_w': gate_w, 'w1': w1, 'b1': b1, 'w2': w2, 'b2': b2, 'sw1': sw1, 'sb1': sb1, 'sw2': sw2, 'sb2': sb2}
    _L0_ffn_in = _L0_ffn_setup()
    _d = {'L0_attn_x': _L0_attn_in['x'], 'L0_attn_W_attn': _L0_attn_in['W_attn'], 'L0_attn_b_attn': _L0_attn_in['b_attn'], 'L0_attn_W_proj': _L0_attn_in['W_proj'], 'L0_attn_b_proj': _L0_attn_in['b_proj'], 'L0_attn_rel_emb': _L0_attn_in['rel_emb'], 'L0_ffn_gate_w': _L0_ffn_in['gate_w'], 'L0_ffn_w1': _L0_ffn_in['w1'], 'L0_ffn_b1': _L0_ffn_in['b1'], 'L0_ffn_w2': _L0_ffn_in['w2'], 'L0_ffn_b2': _L0_ffn_in['b2'], 'L0_ffn_sw1': _L0_ffn_in['sw1'], 'L0_ffn_sb1': _L0_ffn_in['sb1'], 'L0_ffn_sw2': _L0_ffn_in['sw2'], 'L0_ffn_sb2': _L0_ffn_in['sb2']}
    _x0 = _d['L0_attn_x']
    _d['L0_attn_x'] = jax.random.normal(jax.random.fold_in(jax.random.key(seed), 1), (4, 1024, 256), dtype=_x0.dtype)
    del _x0
    return _d

def reference(L0_attn_x, L0_attn_W_attn, L0_attn_b_attn, L0_attn_W_proj, L0_attn_b_proj, L0_attn_rel_emb, L0_ffn_gate_w, L0_ffn_w1, L0_ffn_b1, L0_ffn_w2, L0_ffn_b2, L0_ffn_sw1, L0_ffn_sb1, L0_ffn_sw2, L0_ffn_sb2):

    def _L0_attn_ref(x, W_attn, b_attn, W_proj, b_proj, rel_emb):
        import math
        import jax, jax.numpy as jnp
        import numpy as np
        N_EMBD = 256
        N_HEAD = 16
        NUM_BUCKETS = 32
        MAX_DISTANCE = 128

        def _relative_position_bucket(relative_position, num_buckets=NUM_BUCKETS, max_distance=MAX_DISTANCE):
            rp = -jnp.minimum(relative_position, 0)
            max_exact = num_buckets // 2
            is_small = rp < max_exact
            rp_large = max_exact + (jnp.log(rp.astype(jnp.float32) / max_exact + 1e-10) / math.log(max_distance / max_exact) * (num_buckets - max_exact)).astype(jnp.int32)
            rp_large = jnp.minimum(rp_large, num_buckets - 1)
            return jnp.where(is_small, rp, rp_large)
        B, T, C = x.shape
        H = N_HEAD
        D = C // H
        qkv = x @ W_attn.T + b_attn
        q, k, v = jnp.split(qkv, 3, axis=-1)
        q = q.reshape(B, T, H, D).transpose(0, 2, 1, 3)
        k = k.reshape(B, T, H, D).transpose(0, 2, 1, 3)
        v = v.reshape(B, T, H, D).transpose(0, 2, 1, 3)
        pos = jnp.arange(T)
        rel_pos = pos[None, :] - pos[:, None]
        buckets = _relative_position_bucket(rel_pos)
        rel_bias = rel_emb[buckets]
        rel_bias = rel_bias.transpose(2, 0, 1)[None]
        att = jnp.einsum('bhqd,bhkd->bhqk', q, k) * (1.0 / math.sqrt(D))
        att = att + rel_bias
        causal = jnp.tril(jnp.ones((T, T), dtype=bool))
        att = jnp.where(causal[None, None], att, -jnp.inf)
        att = jax.nn.softmax(att, axis=-1)
        y = jnp.einsum('bhqk,bhkd->bhqd', att, v)
        y = y.transpose(0, 2, 1, 3).reshape(B, T, C)
        y = y @ W_proj.T + b_proj
        return y

    def _L0_ffn_ref(x, gate_w, w1, b1, w2, b2, sw1, sb1, sw2, sb2):
        import jax, jax.numpy as jnp
        import numpy as np
        D_MODEL = 256
        HIDDEN = 1024
        N_ROUTING = 2
        B, S, D = x.shape
        xf = x.reshape(-1, D)
        gate_scores = xf @ gate_w.T
        gate_probs = jax.nn.softmax(gate_scores, axis=-1)
        top1 = jnp.argmax(gate_probs, axis=-1)
        one_hot = jax.nn.one_hot(top1, N_ROUTING, dtype=xf.dtype)
        masked = xf[None, :, :] * one_hot.T[:, :, None]
        h = jax.nn.relu(jnp.einsum('end,edh->enh', masked, w1) + b1[:, None, :])
        expert_out = jnp.einsum('enh,ehd->end', h, w2) + b2[:, None, :]
        routing_output = expert_out.sum(axis=0)
        shared = jax.nn.relu(xf @ sw1 + sb1) @ sw2 + sb2
        return (routing_output + shared).reshape(B, S, D)
    x = L0_attn_x
    x = _layernorm(x + _L0_attn_ref(x, L0_attn_W_attn, L0_attn_b_attn, L0_attn_W_proj, L0_attn_b_proj, L0_attn_rel_emb), axis=-1)
    x = _layernorm(x + _L0_ffn_ref(x, L0_ffn_gate_w, L0_ffn_w1, L0_ffn_b1, L0_ffn_w2, L0_ffn_b2, L0_ffn_sw1, L0_ffn_sb1, L0_ffn_sw2, L0_ffn_sb2), axis=-1)
    return x

_drawn_inputs = setup_inputs


def setup_inputs(seed=0):
    import zlib

    import numpy as np

    out = dict(_drawn_inputs(seed))
    spreads = {'L0_attn_b_attn': (0.0, 0.1), 'L0_attn_b_proj': (0.0, 0.1)}
    factors = {'L0_attn_rel_emb': 25.859, 'L0_ffn_b1': 5.17, 'L0_ffn_sb1': 6.774, 'L0_ffn_sb2': 2.81}
    for name, (base, spread) in spreads.items():
        noise = np.random.default_rng([zlib.crc32(name.encode()), seed]).standard_normal(out[name].shape)
        drawn = base * np.exp(spread * noise) if base else spread * noise
        out[name] = jnp.asarray(drawn.astype(out[name].dtype))
    for name, factor in factors.items():
        out[name] = (out[name] * factor).astype(out[name].dtype)
    return out
```

```python
from contextlib import ExitStack

import numpy as np

import concourse.bass as bass
from concourse import mybir

F32 = mybir.dt.float32
F32R = mybir.dt.float32r
I32 = mybir.dt.int32
BF16 = mybir.dt.bfloat16
ALU = mybir.AluOpType
ACT = mybir.ActivationFunctionType
AX = mybir.AxisListType

P = 128
B, T, C = 4, 1024, 256
H, D = 16, 16
HID = 1024
E = 2
KC = C // P
TT = 512
NB = TT // P
TILES = B * T // TT
TPB = T // TT
HC = HID // P
UH = 4
UNITS = H // UH
KB = T // P
BUCKETS = 32
WIN = 2 * P
NPART = 3
STACK = 2 * NPART * D
GUARD = 3
KROWS = STACK + GUARD
EPS = 1e-5
MASKED = -1.0e30
EXP_TOP = 72.0
EXP_BOTTOM = 65.0
NORM_SLACK = 1.015
SELF_SLACK = 0.01

STEPS = []
for half in range(TPB):
    whole, cut = [], []
    for j in range(KB):
        first = P * j - TT * half
        if first <= 0:
            whole.append((j, 0, TT))
        elif first < TT:
            cut.append((j, first, TT - first))
    STEPS += [(half, [(j, q, w, 0)]) for j, q, w in whole]
    a, b_, c = cut
    STEPS += [(half, [(a[0], a[1], a[2], 0), (c[0], c[1], c[2], a[2])]), (half, [(b_[0], b_[1], b_[2], 0)])]
NSTEP = len(STEPS)
HALF_END = [sum(s[0] <= half for s in STEPS) for half in range(TPB)]
PAIRS = UH // 2
SLOTS = 3
PBUFS = 8


def near(step):
    half, blocks = step
    out = []
    for j, q, w, col in blocks:
        first = TT * half + q - P * j
        if first < WIN:
            out.append((col, min(w, WIN - first), first))
    return out


NEAR_STEPS = [s for s in range(NSTEP) if near(STEPS[s])]


def bucket_rows():
    x = np.arange(3 * P) - P
    rp = np.maximum(x, 0)
    exact = BUCKETS // 2
    large = exact + (np.log(rp.astype(np.float32) / np.float32(exact) + np.float32(1e-10))
                     / np.float32(np.log(128 / exact)) * np.float32(BUCKETS - exact)).astype(np.int32)
    bucket = np.where(rp < exact, rp, np.minimum(large, BUCKETS - 1))
    rows = np.zeros((BUCKETS, 3 * P), np.float32)
    rows[bucket, np.arange(3 * P)] += 1
    rows[BUCKETS - 1] -= 1
    return rows


def build(nc, x, w_attn, b_attn, w_proj, b_proj, rel_emb, gate_w, w1, b1, w2, b2, sw1, sb1, sw2, sb2,
          buckets, out):
    with ExitStack() as ctx:
        def sb(name, shape, dt=F32):
            return ctx.enter_context(nc.sbuf_tensor(name, shape, dt))

        def dram(name, shape, dt):
            return nc.dram_tensor(name, shape, dt, kind="Internal").ap()

        x_tiles = x.rearrange("b t c -> (b t) c").rearrange("(n k p) c -> p n k c", k=NB, p=P)
        out_tiles = out.rearrange("b t c -> (b t) c").rearrange("(n k p) c -> p n k c", k=NB, p=P)
        qk_d = dram("qk_d", [B, 2 * KC, NPART, P, T], BF16)
        guard_d = dram("guard_d", [B, GUARD, H, T], BF16)

        ident = sb("ident", [P, P])
        y_t = sb("y_t", [P, KC, B * T])
        wp_hi = sb("wp_hi", [P, KC, C], F32R)
        wp_lo = sb("wp_lo", [P, KC, C], F32R)
        bp_row = sb("bp_row", [P, C])
        slots = ctx.enter_context(nc.psum_tensor("slots", [P, SLOTS, 2, TT], F32))
        o_ps = ctx.enter_context(nc.psum_tensor("o_ps", [P, 2, TT], F32))

        with ExitStack() as held:
            v_all = held.enter_context(nc.sbuf_tensor("v_all", [P, B * KB, C], F32))
            bias_t = held.enter_context(nc.sbuf_tensor("bias_t", [P, H, WIN], F32))
            wide = held.enter_context(nc.sbuf_tensor("wide", [1, 1], I32))
            project_in(nc, slots, o_ps, ident, wp_hi, wp_lo, bp_row, v_all, bias_t, wide, qk_d, guard_d, x_tiles,
                       w_attn, b_attn, w_proj, b_proj, rel_emb, buckets)
            exact_maxima(nc, slots, o_ps, ident, bias_t, wide, qk_d, guard_d)
            attend(nc, slots, o_ps, v_all, bias_t, y_t, qk_d, guard_d)
        feed_forward(nc, ctx, slots, o_ps, ident, y_t, wp_hi, wp_lo, bp_row, x_tiles, out_tiles,
                     gate_w, (sw1, w1), (sb1, b1), (sw2, w2), (sb2, b2))


PRODUCTS = [(0, 0), (0, 1), (1, 0)]


def rolled(eng, last, body):
    body(0, False, True)
    with eng.Fori(1, last) as i:
        body(i, True, True)
    body(last, True, False)


def project_in(nc, slots, o_ps, ident, wp_hi, wp_lo, bp_row, v_all, bias_t, wide, qk_d, guard_d, x_tiles,
               w_attn, b_attn, w_proj, b_proj, rel_emb, buckets):
    HG = H // KC
    with ExitStack() as ctx:
        def sb(name, shape, dt=F32):
            return ctx.enter_context(nc.sbuf_tensor(name, shape, dt))

        def sem(name):
            return ctx.enter_context(nc.semaphore(name))

        wq = [sb("wq_hi", [P, KC, 3 * C], F32R), sb("wq_lo", [P, KC, 3 * C], F32R)]
        stage_w = sb("stage_w", [P, 8, C])
        qkb_row = sb("qkb_row", [2 * KC, P]); qkb_perm = sb("qkb_perm", [2 * KC, P])
        qk_bias = sb("qk_bias", [P, 2 * KC])
        bv_row = sb("bv_row", [P, C])
        bkt = sb("bkt", [BUCKETS, 3 * P]); rel = sb("rel", [BUCKETS, H]); by_dist = sb("by_dist", [H, 3 * P])
        zeros = sb("zeros", [P, B * GUARD * H * T // P], BF16)
        x_in = sb("x_in", [P, 2, NB, C])
        xt = [sb("xt_hi", [P, KC, TT], F32R), sb("xt_lo", [P, KC, TT], F32R)]
        NC = 2 * KC
        qk_f = sb("qk_f", [P, NC, TT])
        qk_r = sb("qk_r", [P, NC, TT])
        parts = sb("parts", [P, 2, NC, NPART, TT], BF16)
        member = sb("member", [P, 32], BF16)
        squares = sb("squares", [P, NC, TT], BF16)
        selfs = sb("selfs", [P, KC, TT], BF16)
        top_norm = sb("top_norm", [P, TILES])
        low_self = sb("low_self", [32 * KC, TILES])
        top = sb("top", [P, 2]); top_bias = sb("top_bias", [H, 1])
        tops = sb("tops", [1, 16]); guard_b = sb("guard_b", [1, 1], BF16)
        one_row = sb("one_row", [1, P])
        fill = sb("fill", [H * TPB, TT], BF16)
        bias_rows = nc.dram_tensor("bias_rows", [P, H, 3 * P], F32, kind="Internal").ap()

        ld_w = sem("ld_w"); ld_small = sem("ld_small"); pool_set = sem("pool_set"); ident_ok = sem("ident_ok")
        dist_ps = sem("dist_ps"); dist_sb = sem("dist_sb"); dist_out = sem("dist_out"); bias_in = sem("bias_in")
        bias_ok = sem("bias_ok"); perm_ok = sem("perm_ok"); qkb_ps = sem("qkb_ps"); qkb_ok = sem("qkb_ok")
        wt_ps = sem("wt_ps"); wt_hi = sem("wt_hi"); wt_lo = sem("wt_lo"); guard_out = sem("guard_out")
        x_ld = [sem("x_ld0"), sem("x_ld1")]
        xt_ps = sem("xt_ps"); xt_h = sem("xt_h"); xt_l = sem("xt_l"); qk_ps = sem("qk_ps"); qk_ev = sem("qk_ev")
        v_ps = sem("v_ps"); v_ev = sem("v_ev"); part1 = sem("part1"); rem1 = sem("rem1"); part2 = sem("part2")
        member_ok = sem("member_ok"); sq_ok = sem("sq_ok"); norm_ps = sem("norm_ps"); normed = sem("normed")
        top_ok = sem("top_ok"); top_ps = sem("top_ps"); wide_ok = sem("wide_ok")
        root_ok = sem("root_ok"); guard_set = sem("guard_set"); guard_ps = sem("guard_ps"); filled = sem("filled")
        part3 = sem("part3"); stored = [sem("parts_out0"), sem("parts_out1")]

        norm_bank = slots[:, 0, 0, :]
        self_bank = slots[0:32 * KC, 0, 1, :]

        def low_of(n):
            return (wq[1][:, :, P * n:P * n + P] if n < 6 else wp_lo[:, :, P * (n - 6):P * (n - 6) + P])

        def high_of(n):
            return (wq[0][:, :, P * n:P * n + P] if n < 6 else wp_hi[:, :, P * (n - 6):P * (n - 6) + P])

        def order(ap, n):
            return ap.rearrange("p k (d h) -> p k d h", h=HG) if n < 4 else ap

        def as_kept(n):
            src = slots[:, n % SLOTS, 0, 0:2 * P].rearrange("p (k o) -> p k o", k=KC)
            return src.rearrange("p k (h d) -> p k d h", h=HG) if n < 4 else src

        with nc.Block() as block:
            @block.sync
            def _(sp):
                sp.dma_start(stage_w[:, 0:6, :], w_attn.rearrange("(n p) c -> p n c", p=P)).then_inc(ld_w, 16)
                sp.dma_start(x_in[:, 0], x_tiles[:, 0]).then_inc(x_ld[0], 16)
                sp.dma_start(x_in[:, 1], x_tiles[:, 1]).then_inc(x_ld[1], 16)
                sp.dma_start(qkb_row[:, :], b_attn[0:2 * C].rearrange("(n p) -> n p", p=P)).then_inc(ld_small, 16)
                sp.dma_start(bv_row[:, :], b_attn[2 * C:3 * C].partition_broadcast(P)).then_inc(ld_small, 16)
                sp.dma_start(bkt[:, :], buckets).then_inc(ld_small, 16)
                sp.dma_start(rel[:, :], rel_emb).then_inc(ld_small, 16)
                sp.dma_start(stage_w[:, 6:8, :], w_proj.rearrange("(n p) c -> p n c", p=P)).then_inc(ld_w, 16)
                sp.dma_start(bp_row[:, :], b_proj.partition_broadcast(P)).then_inc(ld_small, 16)
                sp.wait_ge(pool_set, 1)
                sp.dma_start(guard_d.rearrange("b g h t -> (b g h t)").rearrange("(p n) -> p n", p=P), zeros[:, :]
                             ).then_inc(guard_out, 16)
                sp.wait_ge(dist_sb, 1)
                sp.dma_start(bias_rows.rearrange("p h x -> h p x"),
                             by_dist[:, :].unsqueeze(1).to_broadcast([H, P, 3 * P])).then_inc(dist_out, 16)
                sp.wait_ge(dist_out, 16)
                skew = bass.AP(bias_rows.tensor, P, [[3 * P * H - 1, P], [3 * P, H], [1, WIN]])
                sp.dma_start(bias_t[:, :, :], skew).then_inc(bias_in, 16)

                def body(b, before, after):
                    for t in range(TPB):
                        n = TPB * b + t
                        if after:
                            nxt = at_tile(x_tiles, n + TPB)
                            sp.wait_ge(xt_ps, n + 1)
                            sp.dma_start(x_in[:, t], nxt).then_inc(x_ld[t], 16)
                        for c in range(NC):
                            dst = qk_d[bass.ds(b, 1), c, :, :, TT * t:TT * t + TT].rearrange("o n p t -> p (o n) t")
                            sp.wait_ge(part3, NC * n + c + 1)
                            sp.dma_start(dst, parts[:, t, c]).then_inc(stored[t], 16)
                rolled(sp, B - 1, body)
                for t in range(TPB):
                    sp.wait_ge(stored[t], 16 * NC * B)
                sp.wait_ge(guard_out, 16)
                sp.wait_ge(filled, 1)
                sp.dma_start(guard_d[:, 0].rearrange("b h (a n) -> (h a) b n", a=TPB),
                             fill[:, :].unsqueeze(1).to_broadcast([H * TPB, B, TT])).then_inc(guard_out, 16)
                sp.wait_ge(guard_out, 32)

            @block.gpsimd
            def _(pool):
                pool.memset(zeros[:, :], 0.0).then_inc(pool_set, 1)
                pool.memset(ident[:, :], 0.0).then_inc(pool_set, 1)
                pool.wait_ge(pool_set, 2)
                pool.affine_select(out=ident[:, :], in_=ident[:, :], compare_op=ALU.not_equal, fill=1.0, base=0,
                                   pattern=[[-1, P]], channel_multiplier=1).then_inc(ident_ok, 1)

                def body(b, before, after):
                    for t in range(TPB):
                        for c in range(NC):
                            m = NC * (TPB * b + t) + c
                            pool.wait_ge(part1, m + 1)
                            if t or before:
                                pool.wait_ge(part3, m - NC + 1)
                            pool.tensor_tensor(qk_r[:, c], qk_f[:, c], parts[:, t, c, 0], ALU.subtract).then_inc(rem1, 1)
                rolled(pool, B - 1, body)
                pool.wait_ge(bias_in, 16)
                pool.affine_select(out=bias_t[:, :, :], in_=bias_t[:, :, :], compare_op=ALU.is_ge, fill=MASKED,
                                   base=0, pattern=[[0, H], [1, WIN]], channel_multiplier=-1).then_inc(bias_ok, 1)

            @block.scalar
            def _(act):
                for n in range(8):
                    act.wait_ge(wt_ps, n + 1)
                    nc.scalar.activation(order(high_of(n), n), as_kept(n), ACT.Copy).then_inc(wt_hi, 1)
                act.wait_ge(qkb_ok, 2)

                def second(n, c):
                    act.wait_ge(rem1, NC * n + c + 1)
                    nc.scalar.activation(parts[:, second.t, c, 1], qk_r[:, c], ACT.Copy).then_inc(part2, 1)

                def body(b, before, after):
                    for t in range(TPB):
                        n = TPB * b + t
                        second.t = t
                        act.wait_ge(xt_ps, n + 1)
                        if t or before:
                            act.wait_ge(v_ps, n)
                        nc.scalar.activation(xt[0][:, :, :], slots[:, 0], ACT.Copy).then_inc(xt_h, 1)
                        for c in range(NC):
                            m = NC * n + c
                            act.wait_ge(qk_ps, NC // 2 * n + c // 2 + 1)
                            if t or before:
                                act.wait_ge(part3, m - NC + 1)
                            nc.scalar.activation(qk_f[:, c], slots[:, 1 + c // 2, c % 2], ACT.Identity,
                                                 bias=qk_bias[:, c:c + 1],
                                                 scale=float(D) ** -0.5 if c < KC else 1.0).then_inc(qk_ev, 1)
                            act.wait_ge(qk_ev, m + 1)
                            if c == 0 and before:
                                act.wait_ge(stored[t], 16 * NC * b)
                            nc.scalar.activation(parts[:, t, c, 0], qk_f[:, c], ACT.Copy).then_inc(part1, 1)
                            if c:
                                second(n, c - 1)
                        second(n, NC - 1)
                rolled(act, B - 1, body)
                act.wait_ge(wide_ok, 5)
                nc.scalar.activation(tops[:, 5:6], tops[:, 4:5], ACT.Sqrt).then_inc(root_ok, 1)

            @block.vector
            def _(dve):
                dve.wait_ge(ld_small, 16 * 5)
                dve.tensor_copy(qkb_perm[:, :].rearrange("n (d h) -> n d h", h=HG),
                                qkb_row[:, :].rearrange("n (h d) -> n d h", h=HG)).then_inc(perm_ok, 1)
                dve.wait_ge(dist_ps, 1)
                dve.tensor_copy(by_dist[:, :], o_ps[0:H, 0, 0:3 * P]).then_inc(dist_sb, 1)
                dve.memset(member[:, :], 0.0).then_inc(member_ok, 1)
                dve.wait_ge(ident_ok, 1)
                dve.wait_ge(member_ok, 1)
                dve.tensor_reduce(member[:, 0:HG], ident[:, :].rearrange("p (d h) -> p h d", h=HG), AX.X, ALU.max
                                  ).then_inc(member_ok, 1)
                dve.wait_ge(qkb_ps, 1)
                dve.tensor_copy(qk_bias[:, :], o_ps[:, 1, 0:2 * KC]).then_inc(qkb_ok, 1)
                dve.wait_ge(qkb_ok, 1)
                dve.tensor_scalar(qk_bias[:, 0:KC], qk_bias[:, 0:KC], float(D) ** -0.5, None, ALU.mult).then_inc(qkb_ok, 1)
                for n in range(8):
                    dve.wait_ge(wt_hi, n + 1)
                    dve.tensor_tensor(order(low_of(n), n), as_kept(n), order(high_of(n), n).bitcast(F32), ALU.subtract
                                      ).then_inc(wt_lo, 1)

                def take_norms(n):
                    dve.wait_ge(norm_ps, n + 1)
                    dve.tensor_reduce(top_norm[:, bass.ds(n, 1)], norm_bank, AX.X, ALU.max).then_inc(normed, 1)
                    dve.tensor_reduce(low_self[:, bass.ds(n, 1)], self_bank, AX.X, ALU.min).then_inc(normed, 1)

                def body(b, before, after):
                    for t in range(TPB):
                        n = TPB * b + t
                        dve.wait_ge(xt_h, n + 1)
                        dve.tensor_tensor(xt[1][:, :, :], slots[:, 0], xt[0][:, :, :].bitcast(F32), ALU.subtract
                                          ).then_inc(xt_l, 1)
                        for c in range(NC):
                            dve.wait_ge(part1, NC * n + c + 1)
                            if c == 0 and (t or before):
                                dve.wait_ge(norm_ps, n)
                            dve.tensor_tensor(squares[:, c], parts[:, t, c, 0], parts[:, t, c, 0], ALU.mult
                                              ).then_inc(sq_ok, 1)
                            if c >= KC:
                                dve.tensor_tensor(selfs[:, c - KC], parts[:, t, c - KC, 0], parts[:, t, c, 0], ALU.mult
                                                  ).then_inc(sq_ok, 1)
                            if c == 0 and (t or before):
                                take_norms(n - 1)
                            dve.wait_ge(part2, NC * n + c + 1)
                            dve.tensor_tensor(parts[:, t, c, 2], qk_r[:, c], parts[:, t, c, 1], ALU.subtract
                                              ).then_inc(part3, 1)
                        dve.wait_ge(v_ps, n + 1)
                        dve.tensor_tensor(v_all[:, bass.ds(NB * n, NB), :],
                                          o_ps[:, :, :].rearrange("p a (k c) -> p (a k) c", c=C),
                                          bv_row[:, :].unsqueeze(1).to_broadcast([P, NB, C]), ALU.add).then_inc(v_ev, 1)
                rolled(dve, B - 1, body)
                take_norms(TILES - 1)
                dve.wait_ge(normed, 2 * TILES)
                dve.memset(top[:, :], 0.0).then_inc(top_ok, 1)
                dve.memset(one_row[:, :], 1.0).then_inc(top_ok, 1)
                dve.wait_ge(top_ok, 2)
                dve.tensor_reduce(top[:, 0:1], top_norm[:, :], AX.X, ALU.max).then_inc(top_ok, 1)
                dve.tensor_reduce(top[0:32 * KC, 1:2], low_self[:, :], AX.X, ALU.min).then_inc(top_ok, 1)
                dve.tensor_reduce(top_bias[:, :], by_dist[:, :], AX.X, ALU.max, apply_absolute_value=True).then_inc(top_ok, 1)

                steps = [0]

                def value(i):
                    return tops[:, i:i + 1]

                def done(ins):
                    steps[0] += 1
                    ins.then_inc(wide_ok, 1)
                    dve.wait_ge(wide_ok, steps[0])

                Q2, K2, BIAS, SELF, SQUARE, ROOT, RAW, GUARD_F, LOW1, LOW2, LOW3, FITS = range(12)
                dve.wait_ge(top_ps, 3)
                done(dve.tensor_reduce(value(Q2), slots[0:1, 0, 0, 0:KC * 32], AX.X, ALU.max))
                done(dve.tensor_reduce(value(K2), slots[0:1, 0, 0, KC * 32:2 * KC * 32], AX.X, ALU.max))
                done(dve.tensor_reduce(value(SELF), slots[0:1, 0, 0, P:2 * P], AX.X, ALU.min))
                done(dve.tensor_reduce(value(BIAS), slots[0:1, 0, 1, 0:H], AX.X, ALU.max))
                steps[0] += 1
                dve.tensor_scalar(value(SQUARE), value(Q2), value(K2), NORM_SLACK, ALU.mult, ALU.mult).then_inc(wide_ok, 1)
                dve.wait_ge(root_ok, 1)
                done(dve.tensor_scalar(value(RAW), value(ROOT), value(BIAS), -EXP_TOP, ALU.add, ALU.add))
                done(dve.tensor_scalar(guard_b[:, :], value(RAW), 0.0, -1.0, ALU.max, ALU.mult))
                done(dve.tensor_copy(value(GUARD_F), guard_b[:, :]))
                dve.sem_inc(guard_set, 1)
                done(dve.tensor_scalar(value(LOW1), value(ROOT), SELF_SLACK, value(BIAS), ALU.mult, ALU.add))
                done(dve.tensor_tensor(value(LOW2), value(LOW1), value(SELF), ALU.subtract))
                done(dve.tensor_tensor(value(LOW3), value(LOW2), value(GUARD_F), ALU.subtract))
                done(dve.tensor_scalar(value(FITS), value(LOW3), EXP_BOTTOM, None, ALU.is_le))
                done(dve.tensor_scalar(wide[:, :], value(FITS), -1.0, 1.0, ALU.mult, ALU.add))
                dve.wait_ge(guard_ps, 1)
                dve.tensor_copy(fill[:, :], o_ps[0:H * TPB, 0, 0:1].to_broadcast([H * TPB, TT])).then_inc(filled, 1)

            @block.tensor
            def _(pe):
                pe.wait_ge(ld_small, 16 * 5)
                pe.matmul(o_ps[0:H, 0, 0:3 * P], rel[:, :], bkt[:, :], start=True, stop=True).then_inc(dist_ps, 1)
                pe.wait_ge(ident_ok, 1)
                pe.wait_ge(perm_ok, 1)
                pe.transpose(o_ps[:, 1, 0:2 * KC], qkb_perm[:, :], ident[0:2 * KC, 0:2 * KC]).then_inc(qkb_ps, 1)
                pe.wait_ge(ld_w, 32)
                for n in range(8):
                    if n >= SLOTS:
                        pe.wait_ge(wt_lo, n - SLOTS + 1)
                    for kc in range(KC):
                        ins = pe.transpose(slots[:, n % SLOTS, 0, P * kc:P * kc + P], stage_w[:, n, P * kc:P * kc + P],
                                           ident[:, :])
                    ins.then_inc(wt_ps, 1)
                pe.wait_ge(wt_lo, 8)
                pe.wait_ge(qkb_ok, 1)

                def turn(n, t):
                    pe.wait_ge(x_ld[t], 16 * (n // TPB + 1) if isinstance(n, int) else 16 * (turn.b + 1))
                    if not (isinstance(n, int) and n == 0):
                        pe.wait_ge(xt_l, n)
                    if not (isinstance(n, int) and n <= 1):
                        pe.wait_ge(normed, 2 * (n - 1))
                    for kc in range(KC):
                        for k in range(NB):
                            ins = pe.transpose(slots[:, 0, kc, P * k:P * k + P], x_in[:, t, k, P * kc:P * kc + P], ident[:, :])
                    ins.then_inc(xt_ps, 1)

                def norms(n):
                    pe.wait_ge(sq_ok, (NC + KC) * (n + 1))
                    for c in range(NC):
                        pe.matmul(norm_bank[32 * c:32 * c + 32], member[:, :], squares[:, c], start=True, stop=True)
                    for c in range(KC):
                        ins = pe.matmul(self_bank[32 * c:32 * c + 32], member[:, :], selfs[:, c], start=True, stop=True)
                    ins.then_inc(norm_ps, 1)

                pe.wait_ge(member_ok, 2)
                turn(0, 0)

                def body(b, before, after):
                    for t in range(TPB):
                        n = TPB * b + t
                        pe.wait_ge(xt_l, n + 1)
                        if t or before:
                            norms(n - 1)
                        for c in range(NC):
                            if c % 2 == 0 and (t or before):
                                pe.wait_ge(qk_ev, NC * (n - 1) + c + 2)
                            for i, (a, w) in enumerate(PRODUCTS):
                                for kc in range(KC):
                                    ins = pe.matmul(slots[:, 1 + c // 2, c % 2], wq[w][:, kc, P * c:P * c + P],
                                                    xt[a][:, kc, :], start=(i == 0 and kc == 0),
                                                    stop=(i == 2 and kc == KC - 1))
                            if c % 2:
                                ins.then_inc(qk_ps, 1)
                        if t + 1 < TPB:
                            turn.b = b
                            turn(n + 1, t + 1)
                        elif after:
                            turn.b = b + 1
                            turn(n + 1, 0)
                        if t or before:
                            pe.wait_ge(v_ev, n)
                        for k in range(NB):
                            for i, (a, w) in enumerate(PRODUCTS):
                                for kc in range(KC):
                                    ins = pe.matmul(o_ps[:, k // 2, C * (k % 2):C * (k % 2) + C],
                                                    xt[a][:, kc, P * k:P * k + P], wq[w][:, kc, 2 * C:3 * C],
                                                    start=(i == 0 and kc == 0), stop=(i == 2 and kc == KC - 1))
                        ins.then_inc(v_ps, 1)
                rolled(pe, B - 1, body)
                norms(TILES - 1)
                pe.wait_ge(top_ok, 5)
                for i in range(2):
                    pe.transpose(slots[0:1, 0, 0, P * i:P * i + P], top[:, i:i + 1], ident[:, :]).then_inc(top_ps, 1)
                pe.transpose(slots[0:1, 0, 1, 0:H], top_bias[:, :], ident[0:H, 0:H]).then_inc(top_ps, 1)
                pe.wait_ge(guard_set, 1)
                pe.matmul(o_ps[0:H * TPB, 0, 0:1], one_row[:, 0:H * TPB], tops[:, 7:8], start=True, stop=True
                          ).then_inc(guard_ps, 1)


def exact_maxima(nc, slots, o_ps, ident, bias_t, wide, qk_d, guard_d):
    HG = H // KC
    STEPS_C = HG * KB
    PARTS_DMAS = 9
    with ExitStack() as ctx:
        def sb(name, shape, dt=F32):
            return ctx.enter_context(nc.sbuf_tensor(name, shape, dt))

        def sem(name):
            return ctx.enter_context(nc.semaphore(name))

        q_all = sb("q_all", [STACK, UH, T], BF16)
        k_all = sb("k_all", [STACK, UH, T], BF16)
        bias_q = sb("bias_q", [P, H, WIN])
        most = sb("most", [P, H * KB])
        neg = sb("neg", [P, P]); rest = sb("rest", [P, P])
        neg_parts = sb("neg_parts", [P, GUARD, P], BF16)

        turned = sem("turned"); bias_q_ok = sem("bias_q_ok"); all_ld = sem("all_ld"); scored = sem("scored")
        added = sem("added"); maxed = sem("maxed"); most_ps = sem("most_ps"); neg_ok = sem("neg_ok")
        split = sem("split"); rest_ok = sem("rest_ok"); neg_out = sem("neg_out")

        with nc.Block() as block:
            @block.sync
            def _(sp):
                rows = qk_d.rearrange("b c n (d h) t -> b c (n d) h t", h=HG)
                with sp.If(sp.value_load(wide[:, :], min_val=0, max_val=1) != 0):
                    sp.sem_inc(neg_out, 16 * GUARD)
                    with sp.Fori(0, B) as b:
                        with sp.Fori(0, KC) as c:
                            q_rows = rows[bass.ds(b, 1), bass.ds(c, 1)].rearrange("o e r h t -> (o e r) h t")
                            k_rows = rows[bass.ds(b, 1), bass.ds(KC + c, 1)].rearrange("o e r h t -> (o e r) h t")
                            for u in range(HG // UH):
                                sp.wait_ge(scored, STEPS_C * (KC * b + c) + STEPS_C // 2 * u + 1)
                                heads = slice(UH * u, UH * u + UH)
                                to = 0
                                for n in (3, 2, 1):
                                    sp.dma_start(k_all[to:to + D * n], k_rows[0:D * n, heads]).then_inc(all_ld, 16)
                                    to += D * n
                                for r, part in enumerate((0, 0, 0, 1, 1, 2)):
                                    sp.dma_start(q_all[D * r:D * r + D], q_rows[D * part:D * part + D, heads]
                                                 ).then_inc(all_ld, 16)
                        sp.wait_ge(split, GUARD * (b + 1))
                        for part in range(GUARD):
                            sp.dma_start(guard_d[bass.ds(b, 1), part].rearrange("o h (k q) -> (o h k) q", q=P),
                                         neg_parts[:, part]).then_inc(neg_out, 16)
                    sp.wait_ge(neg_out, 16 * GUARD * (B + 1))

            @block.vector
            def _(dve):
                with dve.If(dve.value_load(wide[:, :], min_val=0, max_val=1) != 0):
                    dve.sem_inc(maxed, 2)
                    dve.sem_inc(neg_ok, 1)
                    for i in range(H // UH):
                        dve.wait_ge(turned, i + 1)
                        dve.tensor_copy(bias_q[:, UH * i:UH * i + UH, :],
                                        slots[:, i % 2].rearrange("p a (i x) -> p (a i) x", x=WIN)).then_inc(bias_q_ok, 1)
                    dve.wait_ge(bias_q_ok, H // UH)
                    with dve.Fori(0, B) as b:
                        with dve.Fori(0, KC) as c:
                            for h in range(HG):
                                for qb in range(KB):
                                    k = KB * h + qb
                                    n = STEPS_C * (KC * b + c) + k
                                    row = slots[:, k % 2].rearrange("p a x -> p (a x)")
                                    first = P * max(qb - 1, 0)
                                    width = P * (qb + 1) - first
                                    dve.wait_ge(scored, n + 2)
                                    if k == 0:
                                        dve.wait_ge(neg_ok, b + 1)
                                    dve.tensor_tensor(row[:, first:first + width], row[:, first:first + width],
                                                      bias_q[:, bass.ds(c * HG + h, 1), WIN - width:WIN].rearrange("p o x -> p (o x)"),
                                                      ALU.add).then_inc(added, 1)
                                    dve.wait_ge(added, n + 1)
                                    dve.tensor_reduce(most[:, bass.ds(c * STEPS_C + k, 1)], row[:, 0:P * (qb + 1)],
                                                      AX.X, ALU.max).then_inc(maxed, 1)
                        dve.wait_ge(most_ps, b + 1)
                        dve.tensor_scalar(neg[:, :], o_ps[:, 0, 0:P], -1.0, None, ALU.mult).then_inc(neg_ok, 1)
                        dve.wait_ge(neg_ok, b + 2)
                        dve.wait_ge(neg_out, 16 * GUARD * (b + 1))
                        dve.tensor_copy(neg_parts[:, 0], neg[:, :]).then_inc(split, 1)
                        dve.wait_ge(split, GUARD * b + 1)
                        dve.tensor_tensor(rest[:, :], neg[:, :], neg_parts[:, 0], ALU.subtract).then_inc(rest_ok, 1)
                        dve.wait_ge(rest_ok, b + 1)
                        dve.tensor_copy(neg_parts[:, 1], rest[:, :]).then_inc(split, 1)
                        dve.wait_ge(split, GUARD * b + 2)
                        dve.tensor_tensor(neg_parts[:, 2], rest[:, :], neg_parts[:, 1], ALU.subtract).then_inc(split, 1)

            @block.tensor
            def _(pe):
                with pe.If(pe.value_load(wide[:, :], min_val=0, max_val=1) != 0):
                    pe.sem_inc(scored, 1)
                    for i in range(H // UH):
                        if i >= 2:
                            pe.wait_ge(bias_q_ok, i - 1)
                        for h in range(UH):
                            for side in range(2):
                                col = WIN * (h % 2) + P * (1 - side)
                                ins = pe.transpose(slots[:, i % 2, h // 2, col:col + P],
                                                   bias_t[:, UH * i + h, P * side:P * side + P], ident[:, :])
                        ins.then_inc(turned, 1)
                    pe.wait_ge(bias_q_ok, H // UH)
                    with pe.Fori(0, B) as b:
                        with pe.Fori(0, KC) as c:
                            for h in range(HG):
                                if h % UH == 0:
                                    pe.wait_ge(all_ld, 16 * PARTS_DMAS * (2 * (KC * b + c) + h // UH + 1))
                                for qb in range(KB):
                                    k = KB * h + qb
                                    pe.wait_ge(maxed, STEPS_C * (KC * b + c) + k + 1)
                                    for a in range(qb // NB + 1):
                                        w = min(P * (qb + 1) - TT * a, TT)
                                        ins = pe.matmul(slots[:, k % 2, a, 0:w], q_all[:, h % UH, P * qb:P * qb + P],
                                                        k_all[:, h % UH, TT * a:TT * a + w], start=True, stop=True)
                                    ins.then_inc(scored, 1)
                        pe.wait_ge(maxed, KC * STEPS_C * (b + 1) + 2)
                        pe.wait_ge(neg_ok, b + 1)
                        pe.transpose(o_ps[:, 0, 0:P], most[:, :], ident[:, :]).then_inc(most_ps, 1)


def attend(nc, slots, o_ps, v_all, bias_t, y_t, qk_d, guard_d):
    with ExitStack() as ctx:
        def sb(name, shape, dt=F32):
            return ctx.enter_context(nc.sbuf_tensor(name, shape, dt))

        def sem(name):
            return ctx.enter_context(nc.semaphore(name))

        v_st = sb("v_st", [P, UNITS, KB, UH, 2 * D])
        q_st = sb("q_st", [P, 2, UH, T], BF16)
        k_st = sb("k_st", [P, 2, UH, T], BF16)
        probs = sb("probs", [P, PBUFS, 2, TT])
        o_sb = sb("o_sb", [P, UNITS, T])
        sums = sb("sums", [UH * UNITS * KB, P])
        rsums = sb("rsums", [UH * UNITS * KB, P])
        rs_row = sb("rs_row", [P, KC, T])
        rsum_d = nc.dram_tensor("rsum_d", [UH, UNITS, T], F32, kind="Internal").ap()

        ones_ok = sem("ones_ok"); kones_ok = sem("kones_ok"); v_in = sem("v_in")
        st_ld = [sem("st_ld0"), sem("st_ld1")]
        s_ps = sem("s_ps"); biased = sem("biased"); exped = sem("exped"); pv_read = sem("pv_read"); o_ev = sem("o_ev")
        y_out = sem("y_out"); sum_in = sem("sum_in"); rsum_ok = sem("rsum_ok"); rs_out = sem("rs_out")
        rs_in = sem("rs_in"); y_norm = sem("y_norm"); passed = sem("passed_b")

        SU = NSTEP * PAIRS
        SB = SU * UNITS
        ST_DMAS = 10
        NEAR_U = len(NEAR_STEPS) * PAIRS
        HG = H // KC
        KEEP = 8

        with nc.Block() as block:
            @block.sync
            def _(sp):
                rows = qk_d.rearrange("b c n (d h) t -> b c (n d) h t", h=HG)

                def load_stacks(b, g):
                    buf, h0 = g % 2, UH * (g % 2)
                    q_rows = rows[bass.ds(b, 1), g // 2].rearrange("o r h t -> (o r) h t")
                    k_rows = rows[bass.ds(b, 1), KC + g // 2].rearrange("o r h t -> (o r) h t")
                    guards = guard_d[bass.ds(b, 1)].rearrange("o g h t -> (o g) h t")
                    if g >= 2:
                        sp.wait_ge(s_ps, SB * b + SU * (g - 1))
                    elif not (isinstance(b, int) and b == 0):
                        sp.wait_ge(s_ps, SB * b - SU * (1 - g))
                    to = 0
                    for n in (3, 2, 1):
                        sp.dma_start(k_st[to:to + D * n, buf], k_rows[0:D * n, h0:h0 + UH]).then_inc(st_ld[buf], 16)
                        to += D * n
                    for r, part in enumerate((0, 0, 0, 1, 1, 2)):
                        sp.dma_start(q_st[D * r:D * r + D, buf], q_rows[D * part:D * part + D, h0:h0 + UH]
                                     ).then_inc(st_ld[buf], 16)
                    sp.dma_start(q_st[STACK:KROWS, buf], guards[:, UH * g:UH * g + UH]).then_inc(st_ld[buf], 16)

                def move_outputs(b):
                    dst = sp.snap(b * T) if not isinstance(b, int) else b * T
                    sp.wait_ge(o_ev, 2 * UNITS * (b + 1))
                    for j in range(UH):
                        sp.dma_start(sums[UNITS * KB * j:UNITS * KB * (j + 1), :],
                                     o_sb[32 * j + D:32 * j + D + 1].rearrange("o g (k q) -> o (g k) q", q=P)
                                     ).then_inc(sum_in, 16)
                    for j in range(UH):
                        for g2 in range(2):
                            base = D * (UH * g2 + j)
                            sp.dma_start(y_t[base:base + D, :, bass.ds(dst, T)],
                                         o_sb[32 * j:32 * j + D, g2::2, :]).then_inc(y_out, 16)
                    sp.wait_ge(rsum_ok, b + 1)
                    sp.dma_start(rsum_d.rearrange("j g (k q) -> (j g k) q", q=P), rsums[:, :]).then_inc(rs_out, 16)
                    sp.wait_ge(rs_out, 16 * (b + 1))
                    sp.wait_ge(y_norm, b + 1)
                    for j in range(UH):
                        for g2 in range(2):
                            base = D * (UH * g2 + j)
                            sp.dma_start(rs_row[base:base + D], rsum_d[j, g2::2, :].partition_broadcast(D)
                                         ).then_inc(rs_in, 16)

                sp.wait_ge(kones_ok, 2)
                load_stacks(0, 0)
                load_stacks(0, 1)

                def body(b, before, after):
                    if before:
                        move_outputs(b - 1)
                    load_stacks(b, 2)
                    load_stacks(b, 3)
                    if after:
                        load_stacks(b + 1, 0)
                        load_stacks(b + 1, 1)
                rolled(sp, B - 1, body)
                move_outputs(B - 1)

            @block.gpsimd
            def _(pool):
                pool.memset(k_st[STACK:KROWS], 1.0).then_inc(kones_ok, 1)
                pool.wait_ge(kones_ok, 1)
                pool.sem_inc(kones_ok, 1)
                pool.sem_inc(y_norm, 1)

                def divide(b):
                    pool.wait_ge(rs_in, 16 * KEEP * (b + 1))
                    pool.wait_ge(y_out, 16 * KEEP * (b + 1))
                    y = y_t[:, :, bass.ds(b * T, T)]
                    pool.tensor_tensor(y, y, rs_row[:, :, :], ALU.mult).then_inc(y_norm, 1)

                def body(b, before, after):
                    if before:
                        divide(b - 1)
                rolled(pool, B - 1, body)
                divide(B - 1)

            @block.scalar
            def _(act):
                def body(b, before, after):
                    for g in range(UNITS):
                        for s in range(NSTEP):
                            w = sum(x_[2] for x_ in STEPS[s][1])
                            for pair in range(PAIRS):
                                k = SU * g + PAIRS * s + pair
                                if s in NEAR_STEPS:
                                    act.wait_ge(biased, NEAR_U * (UNITS * b + g) + PAIRS * NEAR_STEPS.index(s) + pair + 1)
                                else:
                                    act.wait_ge(s_ps, SB * b + k + 1)
                                if k >= PBUFS or before:
                                    act.wait_ge(pv_read, SB * b + k - PBUFS + 1)
                                nc.scalar.activation(probs[:, k % PBUFS, :, 0:w], slots[:, k % SLOTS, :, 0:w],
                                                     ACT.Exp).then_inc(exped, 1)
                rolled(act, B - 1, body)

            @block.vector
            def _(dve):
                dve.memset(v_st[:, :, :, :, :].rearrange("p g k h d -> p (g k h) d")[:, :, D:2 * D], 1.0).then_inc(ones_ok, 1)

                def load_v(b, g):
                    src = v_all[:, bass.ds(KB * b, KB), UH * D * g:UH * D * (g + 1)]
                    dve.tensor_copy(v_st[:, g, :, :, 0:D], src.rearrange("p k (h d) -> p k h d", d=D)).then_inc(v_in, 1)

                def evacuate(b, g, half):
                    dve.wait_ge(pv_read, SB * b + SU * g + PAIRS * HALF_END[half])
                    if g == 0 and half == 0 and not (isinstance(b, int) and b == 0):
                        dve.wait_ge(y_out, 16 * KEEP * b)
                        dve.wait_ge(sum_in, 16 * UH * b)
                    dve.tensor_copy(o_sb[:, g, TT * half:TT * half + TT], o_ps[:, half]).then_inc(o_ev, 1)

                def invert(b):
                    dve.wait_ge(sum_in, 16 * UH * (b + 1))
                    dve.wait_ge(y_norm, b + 1)
                    dve.reciprocal(rsums[:, :], sums[:, :]).then_inc(rsum_ok, 1)

                for g in range(UNITS):
                    load_v(0, g)

                def body(b, before, after):
                    for g in range(UNITS):
                        for s in range(NSTEP):
                            if s in NEAR_STEPS:
                                for pair in range(PAIRS):
                                    k = SU * g + PAIRS * s + pair
                                    dve.wait_ge(s_ps, SB * b + k + 1)
                                    h0 = UH * g + 2 * pair
                                    for col, w, first in near(STEPS[s]):
                                        tile = slots[:, k % SLOTS, :, col:col + w]
                                        ins = dve.tensor_tensor(tile, tile, bias_t[:, h0:h0 + 2, first:first + w], ALU.add)
                                    ins.then_inc(biased, 1)
                            if s == 1 and g >= 1:
                                evacuate(b, g - 1, 1)
                                if after:
                                    load_v(b + 1, g - 1)
                            if s == 1 and g == 0 and before:
                                evacuate(b - 1, UNITS - 1, 1)
                                load_v(b, UNITS - 1)
                            if s == 4:
                                evacuate(b, g, 0)
                            if s == 2 and g == 0 and before:
                                invert(b - 1)
                rolled(dve, B - 1, body)
                evacuate(B - 1, UNITS - 1, 1)
                invert(B - 1)

            @block.tensor
            def _(pe):
                def scores(b, i, first):
                    g, s = i // NSTEP, i % NSTEP
                    half, blocks = STEPS[s]
                    buf = g % 2
                    if s == 0:
                        pe.wait_ge(st_ld[buf], 16 * ST_DMAS * (2 * b + g // 2 + 1))
                    for pair in range(PAIRS):
                        k = PAIRS * i + pair
                        if k >= SLOTS:
                            pe.wait_ge(exped, SB * b + k - SLOTS + 1)
                        elif not first:
                            last = max(x_ for x_ in range(SB) if x_ % SLOTS == k)
                            pe.wait_ge(exped, SB * b - SB + last + 1)
                        for h in range(2):
                            j2 = 2 * pair + h
                            for j, q, w, col in blocks:
                                q0 = TT * half + q
                                ins = pe.matmul(slots[:, k % SLOTS, h, col:col + w],
                                                k_st[0:KROWS, buf, j2, P * j:P * j + P],
                                                q_st[0:KROWS, buf, j2, q0:q0 + w], start=True, stop=True)
                        ins.then_inc(s_ps, 1)

                def outputs(b, i, before):
                    g, s = i // NSTEP, i % NSTEP
                    half, blocks = STEPS[s]
                    k = PAIRS * i
                    first = s == 0 or STEPS[s - 1][0] != half
                    last = s == NSTEP - 1 or STEPS[s + 1][0] != half
                    if first:
                        if s == 0:
                            pe.wait_ge(v_in, UNITS * b + g + 1)
                        if before or g:
                            pe.wait_ge(o_ev, 2 * (UNITS * b + g) + half - 1)
                    pe.wait_ge(exped, SB * b + k + PAIRS)
                    for i2, (j, q, w, col) in enumerate(blocks):
                        for j2 in range(UH):
                            ins = pe.matmul(o_ps[32 * j2:32 * j2 + 2 * D, half, q:q + w], v_st[:, g, j, j2, :],
                                            probs[:, (k + j2 // 2) % PBUFS, j2 % 2, col:col + w],
                                            start=first and i2 == 0, stop=last and i2 == len(blocks) - 1)
                            if i2 == len(blocks) - 1 and j2 % 2:
                                ins.then_inc(pv_read, 1)

                pe.wait_ge(kones_ok, 1)
                pe.wait_ge(ones_ok, 1)
                scores(0, 0, True)

                def body(b, before, after):
                    for i in range(UNITS * NSTEP):
                        if i + 1 < UNITS * NSTEP:
                            scores(b, i + 1, not before)
                        elif after:
                            scores(b + 1, 0, False)
                        outputs(b, i, before)
                rolled(pe, B - 1, body)


def feed_forward(nc, ctx, slots, o_ps, ident, y_t, wp_hi, wp_lo, bp_row, x_tiles, out_tiles,
                 gate_w, w1s, b1s, w2s, b2s):
    def sb(name, shape, dt=F32):
        return ctx.enter_context(nc.sbuf_tensor(name, shape, dt))

    def sem(name):
        return ctx.enter_context(nc.semaphore(name))

    M = 1 + E
    NQ = M * HC
    w1_d = [w1s[0]] + [w1s[1][e] for e in range(E)]
    w2_d = [w2s[0]] + [w2s[1][e] for e in range(E)]
    b1_d = [b1s[0]] + [b1s[1][e] for e in range(E)]
    b2_d = [b2s[0]] + [b2s[1][e] for e in range(E)]
    w1_hi = sb("w1_hi", [P, M, KC, HID], F32R); w1_lo = sb("w1_lo", [P, M, KC, HID], F32R)
    w2_hi = sb("w2_hi", [P, M, HC, C], F32R); w2_lo = sb("w2_lo", [P, M, HC, C], F32R)
    stage = sb("stage", [P, 2, HID])
    b1_c = sb("b1_c", [P, M, HC])
    rb_hi = sb("rb_hi", [P, E, HC], F32R); rb_lo = sb("rb_lo", [P, E, HC], F32R)
    rb_f = sb("rb_f", [P, E, HC])
    b2_r = sb("b2_r", [P, M, C])
    base0 = sb("base0", [P, C])
    dbase = sb("dbase", [P, C])
    gate_r = sb("gate_r", [P, E, C])
    junk = sb("junk", [P, C]); x1k = sb("x1k", [P, NB, C]); eps_c = sb("eps_c", [P, 1])
    x_sb = sb("x_sb", [P, NB, C])
    yh = sb("yh", [P, KC, TT], F32R); yl = sb("yl", [P, KC, TT], F32R)
    x1 = sb("x1", [P, NB, C])
    xt_hi = sb("x1t_hi", [P, KC, TT], F32R); xt_lo = sb("x1t_lo", [P, KC, TT], F32R)
    base = sb("base", [P, NB, C]); y2 = sb("y2", [P, NB, C]); o_out = sb("o_out", [P, NB, C])
    h_f = sb("h_f", [P, 2, TT]); h_hi = sb("h_hi", [P, 3, TT], F32R); h_lo = sb("h_lo", [P, 3, TT], F32R)
    stats = sb("stats", [P, NB, 6]); mv = sb("mv", [P, NB, 2]); sd = sb("sd", [P, NB]); rstd = sb("rstd", [P, NB])
    stats2 = sb("stats2", [P, NB, 6]); mv2 = sb("mv2", [P, NB, 2]); sd2 = sb("sd2", [P, NB]); rstd2 = sb("rstd2", [P, NB])
    score = sb("score", [P, E, NB]); of1 = sb("of1", [P, NB])
    mask = sb("mask", [P, E, NB])

    ld_stage = [sem("ld_stage0"), sem("ld_stage1")]
    ld_row = sem("ld_row"); w_hi_ok = sem("w_hi_ok"); w_lo_ok = sem("w_lo_ok"); rb_ok = sem("rb_ok"); rbh_ok = sem("rbh_ok")
    rbl_ok = sem("rbl_ok"); const_ps = sem("const_ps"); const_ok = sem("const_ok")
    x_ld2 = sem("x_ld2"); yh_ok = sem("yh_ok"); yl_ok = sem("yl_ok"); xb_ok = sem("xb_ok"); proj_ps = sem("proj_ps")
    r_ok = sem("r_ok"); st_ok = sem("st_ok"); mv_ok = sem("mv_ok"); sd_ok = sem("sd_ok"); rstd_ok = sem("rstd_ok")
    x1_ok = sem("x1_ok"); xt_ps2 = sem("xt_ps2"); xh_ok = sem("xh_ok"); xl_ok = sem("xl_ok")
    eps_ok = sem("eps_ok"); passed = sem("passed_2"); sum_ok = sem("sum_ok"); mask_ok = sem("mask_ok"); score_ok = sem("score_ok"); m_ok = sem("m_ok"); x1k_ok = sem("x1k_ok"); base_ok = sem("base_ok")
    l1_ps = sem("l1_ps"); hf_ok = sem("hf_ok"); hh_ok = sem("hh_ok"); hl_ok = sem("hl_ok"); l2_done = sem("l2_done")
    acc_ok = sem("acc_ok"); st2_ok = sem("st2_ok"); mv2_ok = sem("mv2_ok"); sd2_ok = sem("sd2_ok")
    rstd2_ok = sem("rstd2_ok"); o_ok = sem("o_ok"); stored = sem("stored")

    NW = M * 4
    l1_bank = [slots[:, 0, 0], slots[:, 0, 1]]
    acc_bank = [slots[:, 2, 0, 0:C], slots[:, 2, 1, 0:C], o_ps[:, 0, 0:C], o_ps[:, 1, 0:C]]
    two_banks = slots[:, 1]

    def piece(n, part):
        m, k = n // 4, n % 4
        if k < 2:
            return (w1_hi, w1_lo)[part][:, m, k, :]
        return (w2_hi, w2_lo)[part][:, m, NB * (k - 2):NB * (k - 2) + NB, :].rearrange("p k c -> p (k c)")

    LAST = TILES - 1
    LN1_AT, T_AT, LN2_AT, PROJ_AT = 11, NQ - 3, 4, 8

    def tiles(eng, body):
        rolled(eng, LAST, body)

    with nc.Block() as block:
        @block.sync
        def _(sp):
            sp.sem_inc(stored, 16)
            for n in range(NW):
                m, k = n // 4, n % 4
                if n >= 2:
                    sp.wait_ge(w_lo_ok, n - 1)
                if k < 2:
                    sp.dma_start(stage[:, n % 2, :], w1_d[m][P * k:P * k + P, :]).then_inc(ld_stage[n % 2], 16)
                else:
                    src = w2_d[m][TT * (k - 2):TT * (k - 2) + TT, :].rearrange("(k p) c -> p k c", p=P)
                    sp.dma_start(stage[:, n % 2, :].rearrange("p (k c) -> p k c", c=C), src).then_inc(ld_stage[n % 2], 16)
                if n == 1:
                    for i in range(M):
                        sp.dma_start(b1_c[:, i, :], b1_d[i].rearrange("(k p) -> p k", p=P),
                                     allow_slow_non_contiguous=True).then_inc(ld_row, 16)
                        sp.dma_start(b2_r[:, i, :], b2_d[i].partition_broadcast(P)).then_inc(ld_row, 16)
                    for e in range(E):
                        sp.dma_start(gate_r[:, e, :], gate_w[e].partition_broadcast(P)).then_inc(ld_row, 16)
                    sp.dma_start(x_sb[:, :, :], x_tiles[:, 0]).then_inc(x_ld2, 16)

            def load_x(t):
                sp.wait_ge(r_ok, t)
                sp.dma_start(x_sb[:, :, :], at_tile(x_tiles, t)).then_inc(x_ld2, 16)

            def store(t):
                sp.wait_ge(o_ok, NB * (t + 1))
                sp.dma_start(at_tile(out_tiles, t), o_out[:, :, :]).then_inc(stored, 16)

            def body(t, before, after):
                if after:
                    load_x(t + 1)
                if before:
                    store(t - 1)

            tiles(sp, body)
            store(LAST)
            sp.wait_ge(stored, 16 * (TILES + 1))

        @block.gpsimd
        def _(pool):
            def prepare(t):
                pool.wait_ge(x_ld2, 16 * (t + 1))
                pool.tensor_tensor(x_sb[:, :, :], x_sb[:, :, :], bp_row[:, :].unsqueeze(1).to_broadcast([P, NB, C]),
                                   ALU.add).then_inc(xb_ok, 1)
                pool.wait_ge(yh_ok, t + 1)
                pool.tensor_tensor(yl[:, :, :], y_t[:, :, token(t)], yh[:, :, :].bitcast(F32), ALU.subtract).then_inc(yl_ok, 1)
                pool.wait_ge(x1_ok, NB * (t + 1))
                pool.wait_ge(base_ok, NB * t)
                pool.wait_ge(const_ok, 1)
                pool.tensor_tensor(x1k[:, :, :], x1[:, :, :], base0[:, :].unsqueeze(1).to_broadcast([P, NB, C]),
                                   ALU.add).then_inc(x1k_ok, 1)

            prepare(0)

            def body(t, before, after):
                if after:
                    prepare(t + 1)
            tiles(pool, body)

        @block.scalar
        def _(act):
            for n in range(NW):
                act.wait_ge(ld_stage[n % 2], 16 * (n // 2 + 1))
                nc.scalar.activation(piece(n, 0), stage[:, n % 2, :], ACT.Copy).then_inc(w_hi_ok, 1)
                if n == 1:
                    act.wait_ge(ld_row, 16 * (2 * M + E))
                    nc.scalar.activation(rb_f[:, :, :], b1_c[:, 1:M, :], ACT.Relu).then_inc(rb_ok, 1)
                    act.wait_ge(rb_ok, 1)
                    nc.scalar.activation(rb_hi[:, :, :], rb_f[:, :, :], ACT.Copy).then_inc(rbh_ok, 1)

            def high_y(t):
                act.wait_ge(proj_ps, t)
                nc.scalar.activation(yh[:, :, :], y_t[:, :, token(t)], ACT.Copy).then_inc(yh_ok, 1)

            def root1(t):
                act.wait_ge(mv_ok, NB * (t + 1))
                nc.scalar.activation(sd[:, :], mv[:, :, 1], ACT.Sqrt, bias=eps_c[:, 0:1]).then_inc(sd_ok, 1)

            def high_x1(t):
                act.wait_ge(xt_ps2, t + 1)
                act.wait_ge(l1_ps, NQ * t)
                nc.scalar.activation(xt_hi[:, :, :], two_banks, ACT.Copy).then_inc(xh_ok, 1)

            def root2(t):
                act.wait_ge(mv2_ok, NB * (t + 1))
                nc.scalar.activation(sd2[:, :], mv2[:, :, 1], ACT.Sqrt, bias=eps_c[:, 0:1]).then_inc(sd2_ok, 1)

            act.wait_ge(eps_ok, 1)
            high_y(0)
            root1(0)
            high_x1(0)

            def body(t, before, after):
                for q in range(NQ):
                    n = NQ * t + q
                    act.wait_ge(l1_ps, n + 1)
                    if q >= 2 or before:
                        act.wait_ge(hl_ok, n - 1)
                    nc.scalar.activation(h_f[:, q % 2], l1_bank[q % 2], ACT.Relu,
                                         bias=b1_c[:, q // HC, q % HC:q % HC + 1]).then_inc(hf_ok, 1)
                    act.wait_ge(hf_ok, n + 1)
                    if q >= 3 or before:
                        act.wait_ge(l2_done, n - 2)
                    nc.scalar.activation(h_hi[:, q % 3], h_f[:, q % 2], ACT.Copy).then_inc(hh_ok, 1)
                    if q == LN2_AT and before:
                        root2(t - 1)
                    if q == PROJ_AT - 4 and after:
                        high_y(t + 1)
                    if q == LN1_AT + 1 and after:
                        root1(t + 1)
                if after:
                    high_x1(t + 1)
            tiles(act, body)
            root2(LAST)

        @block.vector
        def _(dve):
            dve.memset(eps_c[:, :], EPS).then_inc(eps_ok, 1)
            for n in range(NW):
                dve.wait_ge(w_hi_ok, n + 1)
                dve.tensor_tensor(piece(n, 1), stage[:, n % 2, :], piece(n, 0).bitcast(F32), ALU.subtract).then_inc(w_lo_ok, 1)
                if n == 1:
                    dve.wait_ge(rbh_ok, 1)
                    dve.tensor_tensor(rb_lo[:, :, :], rb_f[:, :, :], rb_hi[:, :, :].bitcast(F32), ALU.subtract).then_inc(rbl_ok, 1)
            dve.tensor_tensor(base0[:, :], b2_r[:, 0], b2_r[:, 1], ALU.add).then_inc(sum_ok, 1)
            dve.wait_ge(sum_ok, 1)
            dve.tensor_tensor(base0[:, :], base0[:, :], b2_r[:, 2], ALU.add).then_inc(sum_ok, 1)
            dve.wait_ge(sum_ok, 2)
            dve.wait_ge(const_ps, 1)
            dve.tensor_copy(junk[:, :], slots[:, 0, 1, 0:C]).then_inc(sum_ok, 1)
            dve.wait_ge(sum_ok, 3)
            dve.tensor_tensor(dbase[:, :], slots[:, 0, 0, 0:C], junk[:, :], ALU.subtract).then_inc(sum_ok, 1)
            dve.wait_ge(sum_ok, 4)
            dve.tensor_tensor(base0[:, :], base0[:, :], junk[:, :], ALU.add).then_inc(const_ok, 1)

            def norm1(t):
                dve.wait_ge(proj_ps, t + 1)
                dve.wait_ge(xb_ok, t + 1)
                if not (isinstance(t, int) and t == 0):
                    dve.wait_ge(x1k_ok, t)
                    dve.wait_ge(xt_ps2, t)
                dve.tensor_tensor(x1[:, :, :], two_banks.rearrange("p a (k c) -> p (a k) c", c=C), x_sb[:, :, :],
                                  ALU.add).then_inc(r_ok, 1)
                dve.wait_ge(r_ok, t + 1)
                for k in range(NB):
                    dve.bn_stats(stats[:, k], x1[:, k]).then_inc(st_ok, 1)
                dve.wait_ge(st_ok, NB * (t + 1))
                dve.sem_inc(passed, 1)
                for k in range(NB):
                    dve.bn_aggr(mv[:, k], stats[:, k]).then_inc(mv_ok, 1)

            def norm1_end(t):
                dve.wait_ge(sd_ok, t + 1)
                dve.reciprocal(rstd[:, :], sd[:, :]).then_inc(rstd_ok, 1)
                dve.wait_ge(rstd_ok, t + 1)
                for k in range(NB):
                    dve.tensor_scalar(x1[:, k], x1[:, k], mv[:, k, 0:1], rstd[:, k:k + 1], ALU.subtract, ALU.mult
                                      ).then_inc(x1_ok, 1)

            def gate(t):
                dve.wait_ge(x1_ok, NB * (t + 1))
                for e in range(E):
                    for k in range(NB):
                        n = E * NB * t + NB * e + k
                        dve.wait_ge(score_ok, n)
                        dve.tensor_tensor_reduce(junk[:, :], x1[:, k], gate_r[:, e], 1.0, 0.0, ALU.mult, ALU.add,
                                                 score[:, e, k:k + 1]).then_inc(score_ok, 1)
                dve.wait_ge(score_ok, E * NB * (t + 1))
                dve.tensor_tensor(of1[:, :], score[:, 1], score[:, 0], ALU.is_gt).then_inc(m_ok, 1)
                dve.wait_ge(m_ok, t + 1)
                dve.wait_ge(x1k_ok, t + 1)
                for k in range(NB):
                    dve.scalar_tensor_tensor(base[:, k], dbase[:, :], of1[:, k:k + 1], x1k[:, k], ALU.mult, ALU.add
                                             ).then_inc(base_ok, 1)

            def take_mask(t):
                dve.wait_ge(m_ok, t + 1)
                dve.wait_ge(acc_ok, NB * M * t)
                dve.tensor_copy(mask[:, 1], of1[:, :]).then_inc(mask_ok, 1)
                dve.tensor_scalar(mask[:, 0], of1[:, :], -1.0, 1.0, ALU.mult, ALU.add).then_inc(mask_ok, 1)
                dve.wait_ge(mask_ok, E * (t + 1))

            def low_x1(t):
                dve.wait_ge(xh_ok, t + 1)
                dve.tensor_tensor(xt_lo[:, :, :], two_banks, xt_hi[:, :, :].bitcast(F32), ALU.subtract).then_inc(xl_ok, 1)

            def gather(t, m):
                for k in range(NB):
                    n = NB * M * t + NB * m + k
                    dve.wait_ge(l2_done, NQ * t + HC * (m + 1))
                    if m == 0:
                        dve.wait_ge(base_ok, NB * (t + 1))
                        dve.tensor_tensor(y2[:, k], acc_bank[k], base[:, k], ALU.add).then_inc(acc_ok, 1)
                    else:
                        dve.wait_ge(acc_ok, n - NB + 1)
                        dve.scalar_tensor_tensor(y2[:, k], acc_bank[k], mask[:, m - 1, k:k + 1], y2[:, k], ALU.mult, ALU.add
                                                 ).then_inc(acc_ok, 1)

            def norm2(t):
                dve.wait_ge(acc_ok, NB * M * (t + 1))
                for k in range(NB):
                    dve.bn_stats(stats2[:, k], y2[:, k]).then_inc(st2_ok, 1)
                dve.wait_ge(st2_ok, NB * (t + 1))
                dve.sem_inc(passed, 1)
                for k in range(NB):
                    dve.bn_aggr(mv2[:, k], stats2[:, k]).then_inc(mv2_ok, 1)

            def norm2_end(t):
                dve.wait_ge(sd2_ok, t + 1)
                dve.reciprocal(rstd2[:, :], sd2[:, :]).then_inc(rstd2_ok, 1)
                dve.wait_ge(rstd2_ok, t + 1)
                dve.wait_ge(stored, 16 * (t + 1))
                for k in range(NB):
                    dve.tensor_scalar(o_out[:, k], y2[:, k], mv2[:, k, 0:1], rstd2[:, k:k + 1], ALU.subtract, ALU.mult
                                      ).then_inc(o_ok, 1)

            norm1(0)
            norm1_end(0)
            gate(0)
            low_x1(0)

            def body(t, before, after):
                if before:
                    gather(t - 1, M - 1)
                take_mask(t)
                for q in range(NQ):
                    n = NQ * t + q
                    dve.wait_ge(hh_ok, n + 1)
                    dve.tensor_tensor(h_lo[:, q % 3], h_f[:, q % 2], h_hi[:, q % 3].bitcast(F32), ALU.subtract).then_inc(hl_ok, 1)
                    if before and q == LN2_AT - 2:
                        norm2(t - 1)
                    if before and q == LN2_AT + 1:
                        norm2_end(t - 1)
                    if q in (HC + 1, 2 * HC + 1):
                        gather(t, q // HC - 1)
                    if after and q == LN1_AT:
                        norm1(t + 1)
                    if after and q == LN1_AT + 2:
                        norm1_end(t + 1)
                    if after and q == LN1_AT + 3:
                        gate(t + 1)
                if after:
                    low_x1(t + 1)
            tiles(dve, body)
            gather(LAST, M - 1)
            norm2(LAST)
            norm2_end(LAST)

        @block.tensor
        def _(pe):
            pe.wait_ge(rbl_ok, 1)
            pe.wait_ge(w_lo_ok, NW)
            for e in range(E):
                for k in range(HC):
                    for i, (a, w) in enumerate(PRODUCTS):
                        ins = pe.matmul(slots[:, 0, e, 0:C],
                                        (rb_hi, rb_lo)[a][:, e, k:k + 1].to_broadcast([P, P]),
                                        (w2_hi, w2_lo)[w][:, 1 + e, k, :],
                                        start=(k == 0 and i == 0), stop=(k == HC - 1 and i == 2))
            ins.then_inc(const_ps, 1)

            def project(t):
                pe.wait_ge(yl_ok, t + 1)
                if not (isinstance(t, int) and t == 0):
                    pe.wait_ge(xl_ok, t)
                for k in range(NB):
                    for i, (a, w) in enumerate(PRODUCTS):
                        for kc in range(KC):
                            ins = pe.matmul(slots[:, 1, k // 2, C * (k % 2):C * (k % 2) + C],
                                            (yh, yl)[a][:, kc, P * k:P * k + P], (wp_hi, wp_lo)[w][:, kc, :],
                                            start=(i == 0 and kc == 0), stop=(i == 2 and kc == KC - 1))
                ins.then_inc(proj_ps, 1)

            def turn(t):
                pe.wait_ge(x1_ok, NB * (t + 1))
                for kc in range(KC):
                    for k in range(NB):
                        ins = pe.transpose(slots[:, 1, kc, P * k:P * k + P], x1[:, k, P * kc:P * kc + P], ident[:, :])
                ins.then_inc(xt_ps2, 1)

            def hidden(t, q, before):
                m, hc = q // HC, q % HC
                n = NQ * t + q
                if q == 0:
                    pe.wait_ge(xl_ok, t + 1)
                if q >= 2 or before:
                    pe.wait_ge(hf_ok, n - 1)
                for i, (a, w) in enumerate(PRODUCTS):
                    for kc in range(KC):
                        ins = pe.matmul(l1_bank[q % 2], (w1_hi, w1_lo)[w][:, m, kc, P * hc:P * hc + P],
                                        (xt_hi, xt_lo)[a][:, kc, :],
                                        start=(i == 0 and kc == 0), stop=(i == 2 and kc == KC - 1))
                ins.then_inc(l1_ps, 1)

            def output(t, q, before):
                m, hc = q // HC, q % HC
                n = NQ * t + q
                pe.wait_ge(hl_ok, n + 1)
                for k in range(NB):
                    if hc == 0 and (m or before):
                        pe.wait_ge(acc_ok, NB * M * t + NB * (m - 1) + k + 1)
                    for i, (a, w) in enumerate(PRODUCTS):
                        ins = pe.matmul(acc_bank[k], (h_hi, h_lo)[a][:, q % 3, P * k:P * k + P],
                                        (w2_hi, w2_lo)[w][:, m, hc, :],
                                        start=(hc == 0 and i == 0), stop=(hc == HC - 1 and i == 2))
                ins.then_inc(l2_done, 1)

            project(0)
            turn(0)

            def body(t, before, after):
                hidden(t, 0, before)
                hidden(t, 1, before)
                for q in range(NQ):
                    if q + 2 < NQ:
                        hidden(t, q + 2, before)
                    if after and q == PROJ_AT:
                        project(t + 1)
                    if after and q == NQ - 2:
                        turn(t + 1)
                    output(t, q, before)
            tiles(pe, body)


def token(t):
    return bass.ds(t * TT, TT)


def at_tile(dram, t):
    return dram[:, bass.ds(t, 1)].rearrange("p n k c -> p (n k) c")


_INS = ['L0_attn_x', 'L0_attn_W_attn', 'L0_attn_b_attn', 'L0_attn_W_proj', 'L0_attn_b_proj', 'L0_attn_rel_emb',
        'L0_ffn_gate_w', 'L0_ffn_w1', 'L0_ffn_b1', 'L0_ffn_w2', 'L0_ffn_b2', 'L0_ffn_sw1', 'L0_ffn_sb1',
        'L0_ffn_sw2', 'L0_ffn_sb2']


def kernel(**inputs):
    from concourse import bacc
    from concourse.bass_utils import run_bass_kernel_spmd

    nc = bacc.Bacc("TRN2", target_bir_lowering=False, num_devices=1)
    arrays, args = {}, []
    for name in _INS:
        arrays[name] = np.ascontiguousarray(inputs[name])
        args.append(nc.dram_tensor(name, arrays[name].shape, F32, kind="ExternalInput").ap())
    arrays["buckets"] = bucket_rows()
    args.append(nc.dram_tensor("buckets", arrays["buckets"].shape, F32, kind="ExternalInput").ap())
    args.append(nc.dram_tensor("out", (B, T, C), F32, kind="ExternalOutput").ap())
    build(nc, *args)
    return run_bass_kernel_spmd(nc, [arrays], core_ids=[0]).results[0]["out"]
```

```python
from contextlib import ExitStack

import numpy as np

import concourse.bass as bass
from concourse import mybir

F32 = mybir.dt.float32
F32R = mybir.dt.float32r
I32 = mybir.dt.int32
BF16 = mybir.dt.bfloat16
ALU = mybir.AluOpType
ACT = mybir.ActivationFunctionType
AX = mybir.AxisListType

P = 128
B, T, C = 4, 1024, 256
H, D = 16, 16
HID = 1024
E = 2
KC = C // P
TT = 512
NB = TT // P
TILES = B * T // TT
TPB = T // TT
HC = HID // P
UH = 4
UNITS = H // UH
KB = T // P
BUCKETS = 32
WIN = 2 * P
NPART = 3
STACK = 2 * NPART * D
GUARD = 3
KROWS = STACK + GUARD
EPS = 1e-5
MASKED = -1.0e30
EXP_TOP = 72.0
EXP_BOTTOM = 65.0
NORM_SLACK = 1.015
SELF_SLACK = 0.01

WHOLE = [[(half, j, 0, TT, 0) for j in range(KB) if P * j <= TT * half] for half in range(TPB)]
WIDE, MIDDLE, NARROW = ([(half, NB * half + i, P * i, TT - P * i, col) for half in range(TPB)]
                        for i, col in ((1, 0), (2, 0), (3, TT - P)))
STEPS = [[x] for x in WHOLE[0]] + [[WIDE[0], NARROW[0]]]
STEPS += [[MIDDLE[0], MIDDLE[1][:4] + (TT // 2,)]]
STEPS += [[x] for x in WHOLE[1]] + [[WIDE[1], NARROW[1]]]
NSTEP = len(STEPS)
HALF_END = [max(s for s in range(NSTEP) if any(x[0] == half for x in STEPS[s])) + 1 for half in range(TPB)]
HALF_START = [min(s for s in range(NSTEP) if any(x[0] == half for x in STEPS[s])) for half in range(TPB)]


def output_pieces():
    summed, out = set(), []
    for s, blocks in enumerate(STEPS):
        pieces = []
        for half, j, q, w, col in blocks:
            at = q
            while at < q + w:
                end = at + P
                while end < q + w and ((half, end) in summed) == ((half, at) in summed) and col + end - q != TT // 2:
                    end += P
                last = s + 1 == HALF_END[half] and (half, j) == [x[:2] for x in blocks if x[0] == half][-1] and end == q + w
                fresh = at == q and not any(x[0] == half for x in summed)
                pieces.append((half, j, at, end - at, col + at - q, fresh, last))
                at = end
            summed |= {(half, x) for x in range(q, q + w, P)}
        out.append(pieces)
    return out


PIECES = output_pieces()
PAIRS = UH // 2
SLOTS = 3
PBUFS = 6


def near(step):
    out = []
    for half, j, q, w, col in step:
        first = TT * half + q - P * j
        if first < WIN:
            out.append((col, min(w, WIN - first), first))
    return out


NEAR_STEPS = [s for s in range(NSTEP) if near(STEPS[s])]


def bucket_rows():
    x = np.arange(3 * P) - P
    rp = np.maximum(x, 0)
    exact = BUCKETS // 2
    large = exact + (np.log(rp.astype(np.float32) / np.float32(exact) + np.float32(1e-10))
                     / np.float32(np.log(128 / exact)) * np.float32(BUCKETS - exact)).astype(np.int32)
    bucket = np.where(rp < exact, rp, np.minimum(large, BUCKETS - 1))
    rows = np.zeros((BUCKETS, 3 * P), np.float32)
    rows[bucket, np.arange(3 * P)] += 1
    rows[BUCKETS - 1] -= 1
    return rows


def build(nc, x, w_attn, b_attn, w_proj, b_proj, rel_emb, gate_w, w1, b1, w2, b2, sw1, sb1, sw2, sb2,
          buckets, out):
    with ExitStack() as ctx:
        def sb(name, shape, dt=F32):
            return ctx.enter_context(nc.sbuf_tensor(name, shape, dt))

        def dram(name, shape, dt):
            return nc.dram_tensor(name, shape, dt, kind="Internal").ap()

        x_tiles = x.rearrange("b t c -> (b t) c").rearrange("(n k p) c -> p n k c", k=NB, p=P)
        out_tiles = out.rearrange("b t c -> (b t) c").rearrange("(n k p) c -> p n k c", k=NB, p=P)
        qk_d = dram("qk_d", [B, 2 * KC, NPART, P, T], BF16)
        guard_d = dram("guard_d", [B, GUARD, H, T], BF16)

        ident = sb("ident", [P, P])
        y_t = sb("y_t", [P, KC, B * T])
        wp_hi = sb("wp_hi", [P, KC, C], F32R)
        wp_lo = sb("wp_lo", [P, KC, C], F32R)
        bp_row = sb("bp_row", [P, C])
        slots = ctx.enter_context(nc.psum_tensor("slots", [P, SLOTS, 2, TT], F32))
        o_ps = ctx.enter_context(nc.psum_tensor("o_ps", [P, 2, TT], F32))

        TILE_BYTES = NB * C * 4
        work_at = region(nc, ctx, "work", 8 * TILE_BYTES)
        shared_at = region(nc, ctx, "shared", 8 * TILE_BYTES)
        v_all = overlay(nc, "v_all", [P, B * KB, C], F32, work_at)
        tile = tile_steps(nc, ctx, slots, ident, y_t, wp_hi, wp_lo, bp_row, work_at, TILE_BYTES, x_tiles,
                          [sb1] + [b1[e] for e in range(E)])
        shared_w = (overlay(nc, "shared_hi", [P, 2, KC * HID], F32R, shared_at),
                    overlay(nc, "shared_lo", [P, 2, KC * HID], F32R, shared_at + 4 * TILE_BYTES))
        shared_raw = overlay(nc, "shared_raw", [P, 2, KC * HID], F32, shared_at + 4 * TILE_BYTES)

        with ExitStack() as held:
            bias_t = held.enter_context(nc.sbuf_tensor("bias_t", [P, H, WIN], F32))
            wide = held.enter_context(nc.sbuf_tensor("wide", [1, 1], I32))
            k_st = held.enter_context(nc.sbuf_tensor("k_st", [P, 2, UH, T], BF16))
            q_first = held.enter_context(nc.sbuf_tensor("q_first", [P, UH, T], BF16))
            st_ld = [held.enter_context(nc.semaphore(f"st_ld{i}")) for i in range(2)]
            project_in(nc, slots, o_ps, ident, wp_hi, wp_lo, bp_row, v_all, shared_at, bias_t, wide, qk_d, guard_d,
                       k_st, q_first, st_ld, x_tiles, w_attn, b_attn, w_proj, b_proj, rel_emb, buckets)
            exact_maxima(nc, slots, o_ps, ident, bias_t, wide, qk_d, guard_d)
            rs_row = ctx.enter_context(nc.sbuf_tensor("rs_row", [P, KC, T], F32, side="right"))
            divide = division(nc, ctx, y_t, rs_row)
            attend(nc, slots, o_ps, v_all, bias_t, y_t, qk_d, guard_d, k_st, q_first, st_ld, shared_at, shared_w,
                   shared_raw, sw1, sw2, tile, divide, rs_row)
        feed_forward(nc, ctx, slots, o_ps, shared_w, shared_raw, out_tiles, gate_w, w1, w2, (sb2, b2), tile, divide)


def load_parts(sp, qk_d, b, g, k_st, q_st, loaded):
    rows = qk_d.rearrange("b c n (d h) t -> b c (n d) h t", d=D)
    heads = slice(UH * (g % 2), UH * (g % 2) + UH)
    q_rows = rows[bass.ds(b, 1), g // 2].rearrange("o r h t -> (o r) h t")
    k_rows = rows[bass.ds(b, 1), KC + g // 2].rearrange("o r h t -> (o r) h t")
    to = 0
    for n in (3, 2, 1):
        sp.dma_start(k_st[to:to + D * n], k_rows[0:D * n, heads]).then_inc(loaded, 16)
        to += D * n
    to = 0
    for part, times in ((0, 3), (1, 2), (2, 1)):
        src = q_rows[D * part:D * part + D, heads].rearrange("d h t -> d (h t)")
        sp.dma_start(q_st[to:to + D * times].rearrange("r h t -> r (h t)"),
                     src.unsqueeze(0).to_broadcast([times, D, UH * T])).then_inc(loaded, 16)
        to += D * times


def region(nc, ctx, name, size):
    at = -(-nc.sbuf_base // 32) * 32
    ctx.enter_context(nc.sbuf_tensor(name, [P, size // 4], F32))
    return at


def overlay(nc, name, shape, dt, at):
    return nc.alloc_sbuf_tensor_at(name, shape, dt, offset=at)


PRODUCTS = [(0, 0), (0, 1), (1, 0)]


def rolled(eng, last, body):
    body(0, False, True)
    with eng.Fori(1, last) as i:
        body(i, True, True)
    body(last, True, False)


def project_in(nc, slots, o_ps, ident, wp_hi, wp_lo, bp_row, v_all, shared_at, bias_t, wide, qk_d, guard_d,
               k_st, q_first, st_ld, x_tiles, w_attn, b_attn, w_proj, b_proj, rel_emb, buckets):
    HG = H // KC
    with ExitStack() as ctx:
        def sb(name, shape, dt=F32):
            return ctx.enter_context(nc.sbuf_tensor(name, shape, dt))

        def sem(name):
            return ctx.enter_context(nc.semaphore(name))

        wq = [sb("wq_hi", [P, KC, 3 * C], F32R), sb("wq_lo", [P, KC, 3 * C], F32R)]
        quarter = 2 * NB * C * 4
        stage_w = overlay(nc, "stage_w", [P, 8, C], F32, shared_at)
        qkb_row = sb("qkb_row", [2 * KC, P]); qkb_perm = sb("qkb_perm", [2 * KC, P])
        qk_bias = sb("qk_bias", [P, 2 * KC])
        bv_row = sb("bv_row", [P, C])
        bkt = sb("bkt", [BUCKETS, 3 * P]); rel = sb("rel", [BUCKETS, H]); by_dist = sb("by_dist", [H, 3 * P])
        zeros = sb("zeros", [P, P], BF16)
        x_in = overlay(nc, "x_in", [P, TPB, NB, C], F32, shared_at + quarter)
        xt = [sb("xt_hi", [P, TPB, KC, TT], F32R), sb("xt_lo", [P, TPB, KC, TT], F32R)]
        NC = 2 * KC
        qk_f = overlay(nc, "qk_f", [P, NC, TT], F32, shared_at + 2 * quarter)
        qk_r = overlay(nc, "qk_r", [P, NC, TT], F32, shared_at + 3 * quarter)
        parts = sb("parts", [P, 2, NC, NPART, TT], BF16)
        member = sb("member", [P, 32], BF16)
        squares = sb("squares", [P, NC, TT], BF16)
        selfs = sb("selfs", [P, KC, TT], BF16)
        top_norm = sb("top_norm", [P, TILES])
        low_self = sb("low_self", [32 * KC, TILES])
        top = sb("top", [P, 2]); top_bias = sb("top_bias", [H, 1])
        tops = sb("tops", [1, 16]); guard_b = sb("guard_b", [1, 1], BF16)
        one_row = sb("one_row", [1, P])
        fill = sb("fill", [H * TPB, TT], BF16)
        bias_rows = nc.dram_tensor("bias_rows", [P, H, 3 * P], F32, kind="Internal").ap()

        ld_w = [sem(f"ld_w{n}") for n in range(4)]
        ld_small = sem("ld_small"); pool_set = sem("pool_set"); ident_ok = sem("ident_ok")
        dist_ps = sem("dist_ps"); dist_sb = sem("dist_sb"); dist_out = sem("dist_out"); bias_in = sem("bias_in")
        bias_ok = sem("bias_ok"); perm_ok = sem("perm_ok"); qkb_ps = sem("qkb_ps"); qkb_ok = sem("qkb_ok")
        wt_ps = sem("wt_ps"); wt_hi = sem("wt_hi"); wt_lo = sem("wt_lo"); guard_out = sem("guard_out")
        x_ld = [sem("x_ld0"), sem("x_ld1")]
        xt_ps = sem("xt_ps"); xt_h = sem("xt_h"); xt_l = sem("xt_l"); qk_ps = sem("qk_ps"); qk_ev = sem("qk_ev")
        v_ps = sem("v_ps"); v_ev = sem("v_ev"); part1 = sem("part1"); rem1 = sem("rem1"); part2 = sem("part2")
        member_ok = sem("member_ok"); sq_ok = sem("sq_ok"); norm_ps = sem("norm_ps"); normed = sem("normed")
        top_ok = sem("top_ok"); top_ps = sem("top_ps"); wide_ok = sem("wide_ok")
        root_ok = sem("root_ok"); guard_set = sem("guard_set"); guard_ps = sem("guard_ps"); filled = sem("filled")
        part3 = sem("part3"); stored = [sem("parts_out0"), sem("parts_out1")]

        norm_bank = slots[:, 0, 0, :]
        self_bank = slots[0:32 * KC, 0, 1, :]

        def low_of(n):
            return (wq[1][:, :, P * n:P * n + P] if n < 6 else wp_lo[:, :, P * (n - 6):P * (n - 6) + P])

        def high_of(n):
            return (wq[0][:, :, P * n:P * n + P] if n < 6 else wp_hi[:, :, P * (n - 6):P * (n - 6) + P])

        def order(ap, n):
            return ap.rearrange("p k (d h) -> p k d h", h=HG) if n < 4 else ap

        def w_place(n):
            return slots[:, 1 + n % 2, n // 2 % 2, 0:2 * P]

        def as_kept(n):
            src = w_place(n).rearrange("p (k o) -> p k o", k=KC)
            return src.rearrange("p k (h d) -> p k d h", h=HG) if n < 4 else src

        with nc.Block() as block:
            @block.sync
            def _(sp):
                w_rows = w_attn.rearrange("(n p) c -> p n c", p=P)
                sp.dma_start(x_in[:, 0], x_tiles[:, 0]).then_inc(x_ld[0], 16)
                for n in range(3):
                    sp.dma_start(stage_w[:, 2 * n:2 * n + 2, :], w_rows[:, 2 * n:2 * n + 2]).then_inc(ld_w[n], 16)
                sp.dma_start(stage_w[:, 6:8, :], w_proj.rearrange("(n p) c -> p n c", p=P)).then_inc(ld_w[3], 16)
                sp.dma_start(qkb_row[:, :], b_attn[0:2 * C].rearrange("(n p) -> n p", p=P)).then_inc(ld_small, 16)
                sp.dma_start(bkt[:, :], buckets).then_inc(ld_small, 16)
                sp.dma_start(rel[:, :], rel_emb).then_inc(ld_small, 16)
                sp.dma_start(bv_row[:, :], b_attn[2 * C:3 * C].partition_broadcast(P)).then_inc(ld_small, 16)
                sp.dma_start(bp_row[:, :], b_proj.partition_broadcast(P)).then_inc(ld_small, 16)
                sp.dma_start(x_in[:, 1], x_tiles[:, 1]).then_inc(x_ld[1], 16)
                sp.wait_ge(pool_set, 1)
                flat = guard_d.rearrange("b g h t -> (b g h t)").rearrange("(p n c) -> p n c", p=P, c=P)
                sp.dma_start(flat, zeros[:, :].unsqueeze(1).to_broadcast([P, B * GUARD * H * T // P // P, P])
                             ).then_inc(guard_out, 16)
                sp.wait_ge(dist_sb, 1)
                sp.dma_start(bias_rows.rearrange("p h x -> h p x"),
                             by_dist[:, :].unsqueeze(1).to_broadcast([H, P, 3 * P])).then_inc(dist_out, 16)
                sp.wait_ge(dist_out, 16)
                skew = bass.AP(bias_rows.tensor, P, [[3 * P * H - 1, P], [3 * P, H], [1, WIN]])
                sp.dma_start(bias_t[:, :, :], skew).then_inc(bias_in, 16)

                def body(b, before, after):
                    for t in range(TPB):
                        n = TPB * b + t
                        if after:
                            nxt = at_tile(x_tiles, n + TPB)
                            sp.wait_ge(xt_ps, n + 1)
                            sp.dma_start(x_in[:, t], nxt).then_inc(x_ld[t], 16)
                        for c in range(NC):
                            dst = qk_d[bass.ds(b, 1), c, :, :, TT * t:TT * t + TT].rearrange("o n p t -> p (o n) t")
                            sp.wait_ge(part3, NC * n + c + 1)
                            sp.dma_start(dst, parts[:, t, c]).then_inc(stored[t], 16)
                rolled(sp, B - 1, body)
                for t in range(TPB):
                    sp.wait_ge(stored[t], 16 * NC * B)
                load_parts(sp, qk_d, 0, 0, k_st[:, 0], q_first, st_ld[0])
                sp.wait_ge(guard_out, 16)
                sp.wait_ge(filled, 1)
                sp.dma_start(guard_d[:, 0].rearrange("b h (a n) -> (h a) b n", a=TPB),
                             fill[:, :].unsqueeze(1).to_broadcast([H * TPB, B, TT])).then_inc(guard_out, 16)
                sp.wait_ge(guard_out, 32)

            @block.gpsimd
            def _(pool):
                pool.memset(zeros[:, :], 0.0).then_inc(pool_set, 1)
                pool.memset(ident[:, :], 0.0).then_inc(pool_set, 1)
                pool.wait_ge(pool_set, 2)
                pool.affine_select(out=ident[:, :], in_=ident[:, :], compare_op=ALU.not_equal, fill=1.0, base=0,
                                   pattern=[[-1, P]], channel_multiplier=1).then_inc(ident_ok, 1)
                pool.wait_ge(ident_ok, 1)
                pool.memset(k_st[STACK:KROWS], 1.0).then_inc(pool_set, 1)
                pool.wait_ge(pool_set, 3)

                def body(b, before, after):
                    for t in range(TPB):
                        for c in range(NC):
                            m = NC * (TPB * b + t) + c
                            pool.wait_ge(part1, m + 1)
                            if t or before:
                                pool.wait_ge(part3, m - NC + 1)
                            pool.tensor_tensor(qk_r[:, c], qk_f[:, c], parts[:, t, c, 0], ALU.subtract).then_inc(rem1, 1)
                rolled(pool, B - 1, body)
                pool.wait_ge(bias_in, 16)
                pool.affine_select(out=bias_t[:, :, :], in_=bias_t[:, :, :], compare_op=ALU.is_ge, fill=MASKED,
                                   base=0, pattern=[[0, H], [1, WIN]], channel_multiplier=-1).then_inc(bias_ok, 1)

            @block.scalar
            def _(act):
                def second(n, c):
                    act.wait_ge(rem1, NC * n + c + 1)
                    nc.scalar.activation(parts[:, second.t, c, 1], qk_r[:, c], ACT.Copy).then_inc(part2, 1)

                def high_x(n, t, waits):
                    act.wait_ge(xt_ps, n + 1)
                    if waits:
                        act.wait_ge(v_ps, n - 1)
                    nc.scalar.activation(xt[0][:, t], slots[:, 0], ACT.Copy).then_inc(xt_h, 1)

                high_x(0, 0, False)
                for n in range(8):
                    act.wait_ge(wt_ps, n + 1)
                    nc.scalar.activation(order(high_of(n), n), as_kept(n), ACT.Copy).then_inc(wt_hi, 1)
                act.wait_ge(qkb_ok, 2)

                def body(b, before, after):
                    for t in range(TPB):
                        n = TPB * b + t
                        second.t = t
                        for c in range(NC):
                            if c == NC - 1 and (t + 1 < TPB or after):
                                high_x(n + 1, (t + 1) % TPB, t or before)
                            m = NC * n + c
                            act.wait_ge(qk_ps, m + 1)
                            if t or before:
                                act.wait_ge(part3, m - NC + 1)
                            nc.scalar.activation(qk_f[:, c], slots[:, 1 + c // 2, c % 2], ACT.Identity,
                                                 bias=qk_bias[:, c:c + 1],
                                                 scale=float(D) ** -0.5 if c < KC else 1.0).then_inc(qk_ev, 1)
                            act.wait_ge(qk_ev, m + 1)
                            if c == 0 and before:
                                act.wait_ge(stored[t], 16 * NC * b)
                            nc.scalar.activation(parts[:, t, c, 0], qk_f[:, c], ACT.Copy).then_inc(part1, 1)
                            if c:
                                second(n, c - 1)
                        second(n, NC - 1)
                rolled(act, B - 1, body)
                act.wait_ge(wide_ok, 5)
                nc.scalar.activation(tops[:, 5:6], tops[:, 4:5], ACT.Sqrt).then_inc(root_ok, 1)

            @block.vector
            def _(dve):
                dve.memset(member[:, :], 0.0).then_inc(member_ok, 1)
                dve.wait_ge(ident_ok, 1)
                dve.wait_ge(member_ok, 1)
                dve.tensor_reduce(member[:, 0:HG], ident[:, :].rearrange("p (d h) -> p h d", h=HG), AX.X, ALU.max
                                  ).then_inc(member_ok, 1)

                def take_norms(n):
                    dve.wait_ge(norm_ps, n + 1)
                    dve.tensor_reduce(top_norm[:, bass.ds(n, 1)], norm_bank, AX.X, ALU.max).then_inc(normed, 1)
                    dve.tensor_reduce(low_self[:, bass.ds(n, 1)], self_bank, AX.X, ALU.min).then_inc(normed, 1)

                def low_x(n, t):
                    dve.wait_ge(xt_h, n + 1)
                    dve.tensor_tensor(xt[1][:, t], slots[:, 0], xt[0][:, t].bitcast(F32), ALU.subtract).then_inc(xt_l, 1)

                def low_w(n):
                    dve.wait_ge(wt_hi, n + 1)
                    dve.tensor_tensor(order(low_of(n), n), as_kept(n), order(high_of(n), n).bitcast(F32), ALU.subtract
                                      ).then_inc(wt_lo, 1)

                low_x(0, 0)
                for n in range(6):
                    low_w(n)
                dve.wait_ge(ld_small, 16 * 5)
                dve.tensor_copy(qkb_perm[:, :].rearrange("n (d h) -> n d h", h=HG),
                                qkb_row[:, :].rearrange("n (h d) -> n d h", h=HG)).then_inc(perm_ok, 1)
                low_w(6)
                low_w(7)
                dve.wait_ge(qkb_ps, 1)
                dve.tensor_copy(qk_bias[:, :], o_ps[:, 1, 0:2 * KC]).then_inc(qkb_ok, 1)
                dve.wait_ge(qkb_ok, 1)
                dve.tensor_scalar(qk_bias[:, 0:KC], qk_bias[:, 0:KC], float(D) ** -0.5, None, ALU.mult).then_inc(qkb_ok, 1)
                dve.wait_ge(dist_ps, 1)
                dve.tensor_copy(by_dist[:, :], o_ps[0:H, 0, 0:3 * P]).then_inc(dist_sb, 1)

                def body(b, before, after):
                    for t in range(TPB):
                        n = TPB * b + t
                        for c in range(NC):
                            dve.wait_ge(part1, NC * n + c + 1)
                            if c == 0 and (t or before):
                                dve.wait_ge(norm_ps, n)
                            dve.tensor_tensor(squares[:, c], parts[:, t, c, 0], parts[:, t, c, 0], ALU.mult
                                              ).then_inc(sq_ok, 1)
                            if c >= KC:
                                dve.tensor_tensor(selfs[:, c - KC], parts[:, t, c - KC, 0], parts[:, t, c, 0], ALU.mult
                                                  ).then_inc(sq_ok, 1)
                            if c == 0 and (t or before):
                                take_norms(n - 1)
                            if c == NC - 2 and (t + 1 < TPB or after):
                                low_x(n + 1, (t + 1) % TPB)
                            dve.wait_ge(part2, NC * n + c + 1)
                            dve.tensor_tensor(parts[:, t, c, 2], qk_r[:, c], parts[:, t, c, 1], ALU.subtract
                                              ).then_inc(part3, 1)
                        dve.wait_ge(v_ps, n + 1)
                        dve.tensor_tensor(v_all[:, bass.ds(NB * n, NB), :],
                                          o_ps[:, :, :].rearrange("p a (k c) -> p (a k) c", c=C),
                                          bv_row[:, :].unsqueeze(1).to_broadcast([P, NB, C]), ALU.add).then_inc(v_ev, 1)
                rolled(dve, B - 1, body)
                take_norms(TILES - 1)
                dve.wait_ge(normed, 2 * TILES)
                dve.memset(top[:, :], 0.0).then_inc(top_ok, 1)
                dve.memset(one_row[:, :], 1.0).then_inc(top_ok, 1)
                dve.wait_ge(top_ok, 2)
                dve.tensor_reduce(top[:, 0:1], top_norm[:, :], AX.X, ALU.max).then_inc(top_ok, 1)
                dve.tensor_reduce(top[0:32 * KC, 1:2], low_self[:, :], AX.X, ALU.min).then_inc(top_ok, 1)
                dve.tensor_reduce(top_bias[:, :], by_dist[:, :], AX.X, ALU.max, apply_absolute_value=True).then_inc(top_ok, 1)

                steps = [0]

                def value(i):
                    return tops[:, i:i + 1]

                def done(ins):
                    steps[0] += 1
                    ins.then_inc(wide_ok, 1)
                    dve.wait_ge(wide_ok, steps[0])

                Q2, K2, BIAS, SELF, SQUARE, ROOT, RAW, GUARD_F, LOW1, LOW2, LOW3, FITS = range(12)
                dve.wait_ge(top_ps, 3)
                done(dve.tensor_reduce(value(Q2), slots[0:1, 0, 0, 0:KC * 32], AX.X, ALU.max))
                done(dve.tensor_reduce(value(K2), slots[0:1, 0, 0, KC * 32:2 * KC * 32], AX.X, ALU.max))
                done(dve.tensor_reduce(value(SELF), slots[0:1, 0, 0, P:2 * P], AX.X, ALU.min))
                done(dve.tensor_reduce(value(BIAS), slots[0:1, 0, 1, 0:H], AX.X, ALU.max))
                steps[0] += 1
                dve.tensor_scalar(value(SQUARE), value(Q2), value(K2), NORM_SLACK, ALU.mult, ALU.mult).then_inc(wide_ok, 1)
                dve.wait_ge(root_ok, 1)
                done(dve.tensor_scalar(value(RAW), value(ROOT), value(BIAS), -EXP_TOP, ALU.add, ALU.add))
                done(dve.tensor_scalar(guard_b[:, :], value(RAW), 0.0, -1.0, ALU.max, ALU.mult))
                done(dve.tensor_copy(value(GUARD_F), guard_b[:, :]))
                dve.sem_inc(guard_set, 1)
                done(dve.tensor_scalar(value(LOW1), value(ROOT), SELF_SLACK, value(BIAS), ALU.mult, ALU.add))
                done(dve.tensor_tensor(value(LOW2), value(LOW1), value(SELF), ALU.subtract))
                done(dve.tensor_tensor(value(LOW3), value(LOW2), value(GUARD_F), ALU.subtract))
                done(dve.tensor_scalar(value(FITS), value(LOW3), EXP_BOTTOM, None, ALU.is_le))
                done(dve.tensor_scalar(wide[:, :], value(FITS), -1.0, 1.0, ALU.mult, ALU.add))
                dve.wait_ge(guard_ps, 1)
                dve.tensor_copy(fill[:, :], o_ps[0:H * TPB, 0, 0:1].to_broadcast([H * TPB, TT])).then_inc(filled, 1)

            @block.tensor
            def _(pe):
                def turn(n, t):
                    pe.wait_ge(x_ld[t], 16 * (n // TPB + 1) if isinstance(n, int) else 16 * (turn.b + 1))
                    if not (isinstance(n, int) and n == 0):
                        pe.wait_ge(xt_l, n)
                    if not (isinstance(n, int) and n <= 1):
                        pe.wait_ge(normed, 2 * (n - 1))
                    for kc in range(KC):
                        for k in range(NB):
                            ins = pe.transpose(slots[:, 0, kc, P * k:P * k + P], x_in[:, t, k, P * kc:P * kc + P], ident[:, :])
                    ins.then_inc(xt_ps, 1)

                def norms(n):
                    pe.wait_ge(sq_ok, (NC + KC) * (n + 1))
                    for c in range(NC):
                        pe.matmul(norm_bank[32 * c:32 * c + 32], member[:, :], squares[:, c], start=True, stop=True)
                    for c in range(KC):
                        ins = pe.matmul(self_bank[32 * c:32 * c + 32], member[:, :], selfs[:, c], start=True, stop=True)
                    ins.then_inc(norm_ps, 1)

                pe.wait_ge(ident_ok, 1)
                turn(0, 0)
                for n in range(8):
                    if n % 2 == 0:
                        pe.wait_ge(ld_w[n // 2], 16)
                    if n >= 4:
                        pe.wait_ge(wt_lo, n - 3)
                    for kc in range(KC):
                        ins = pe.transpose(w_place(n)[:, P * kc:P * kc + P], stage_w[:, n, P * kc:P * kc + P], ident[:, :])
                    ins.then_inc(wt_ps, 1)
                pe.wait_ge(perm_ok, 1)
                pe.transpose(o_ps[:, 1, 0:2 * KC], qkb_perm[:, :], ident[0:2 * KC, 0:2 * KC]).then_inc(qkb_ps, 1)
                pe.wait_ge(ld_small, 16 * 5)
                pe.matmul(o_ps[0:H, 0, 0:3 * P], rel[:, :], bkt[:, :], start=True, stop=True).then_inc(dist_ps, 1)
                pe.wait_ge(wt_lo, 8)
                pe.wait_ge(member_ok, 2)
                pe.wait_ge(dist_sb, 1)

                def body(b, before, after):
                    for t in range(TPB):
                        n = TPB * b + t
                        pe.wait_ge(xt_l, n + 1)
                        for c in range(NC):
                            if c == 1 and (t or before):
                                norms(n - 1)
                            if t or before:
                                pe.wait_ge(qk_ev, NC * (n - 1) + c + 1)
                            for i, (a, w) in enumerate(PRODUCTS):
                                for kc in range(KC):
                                    ins = pe.matmul(slots[:, 1 + c // 2, c % 2], wq[w][:, kc, P * c:P * c + P],
                                                    xt[a][:, t, kc, :], start=(i == 0 and kc == 0),
                                                    stop=(i == 2 and kc == KC - 1))
                            ins.then_inc(qk_ps, 1)
                        if t + 1 < TPB:
                            turn.b = b
                            turn(n + 1, t + 1)
                        elif after:
                            turn.b = b + 1
                            turn(n + 1, 0)
                        if t or before:
                            pe.wait_ge(v_ev, n)
                        for k in range(NB):
                            for i, (a, w) in enumerate(PRODUCTS):
                                for kc in range(KC):
                                    ins = pe.matmul(o_ps[:, k // 2, C * (k % 2):C * (k % 2) + C],
                                                    xt[a][:, t, kc, P * k:P * k + P], wq[w][:, kc, 2 * C:3 * C],
                                                    start=(i == 0 and kc == 0), stop=(i == 2 and kc == KC - 1))
                        ins.then_inc(v_ps, 1)
                rolled(pe, B - 1, body)
                norms(TILES - 1)
                pe.wait_ge(top_ok, 5)
                for i in range(2):
                    pe.transpose(slots[0:1, 0, 0, P * i:P * i + P], top[:, i:i + 1], ident[:, :]).then_inc(top_ps, 1)
                pe.transpose(slots[0:1, 0, 1, 0:H], top_bias[:, :], ident[0:H, 0:H]).then_inc(top_ps, 1)
                pe.wait_ge(guard_set, 1)
                pe.matmul(o_ps[0:H * TPB, 0, 0:1], one_row[:, 0:H * TPB], tops[:, 7:8], start=True, stop=True
                          ).then_inc(guard_ps, 1)


def exact_maxima(nc, slots, o_ps, ident, bias_t, wide, qk_d, guard_d):
    HG = H // KC
    STEPS_C = HG * KB
    PARTS_DMAS = 9
    with ExitStack() as ctx:
        def sb(name, shape, dt=F32):
            return ctx.enter_context(nc.sbuf_tensor(name, shape, dt))

        def sem(name):
            return ctx.enter_context(nc.semaphore(name))

        q_all = sb("q_all", [STACK, UH, T], BF16)
        k_all = sb("k_all", [STACK, UH, T], BF16)
        bias_q = sb("bias_q", [P, H, WIN])
        most = sb("most", [P, H * KB])
        neg = sb("neg", [P, P]); rest = sb("rest", [P, P])
        neg_parts = sb("neg_parts", [P, GUARD, P], BF16)

        turned = sem("turned"); bias_q_ok = sem("bias_q_ok"); all_ld = sem("all_ld"); scored = sem("scored")
        added = sem("added"); maxed = sem("maxed"); most_ps = sem("most_ps"); neg_ok = sem("neg_ok")
        split = sem("split"); rest_ok = sem("rest_ok"); neg_out = sem("neg_out")

        with nc.Block() as block:
            @block.sync
            def _(sp):
                rows = qk_d.rearrange("b c n (d h) t -> b c (n d) h t", h=HG)
                with sp.If(sp.value_load(wide[:, :], min_val=0, max_val=1) != 0):
                    sp.sem_inc(neg_out, 16 * GUARD)
                    with sp.Fori(0, B) as b:
                        with sp.Fori(0, KC) as c:
                            q_rows = rows[bass.ds(b, 1), bass.ds(c, 1)].rearrange("o e r h t -> (o e r) h t")
                            k_rows = rows[bass.ds(b, 1), bass.ds(KC + c, 1)].rearrange("o e r h t -> (o e r) h t")
                            for u in range(HG // UH):
                                sp.wait_ge(scored, STEPS_C * (KC * b + c) + STEPS_C // 2 * u + 1)
                                heads = slice(UH * u, UH * u + UH)
                                to = 0
                                for n in (3, 2, 1):
                                    sp.dma_start(k_all[to:to + D * n], k_rows[0:D * n, heads]).then_inc(all_ld, 16)
                                    to += D * n
                                for r, part in enumerate((0, 0, 0, 1, 1, 2)):
                                    sp.dma_start(q_all[D * r:D * r + D], q_rows[D * part:D * part + D, heads]
                                                 ).then_inc(all_ld, 16)
                        sp.wait_ge(split, GUARD * (b + 1))
                        for part in range(GUARD):
                            sp.dma_start(guard_d[bass.ds(b, 1), part].rearrange("o h (k q) -> (o h k) q", q=P),
                                         neg_parts[:, part]).then_inc(neg_out, 16)
                    sp.wait_ge(neg_out, 16 * GUARD * (B + 1))

            @block.vector
            def _(dve):
                with dve.If(dve.value_load(wide[:, :], min_val=0, max_val=1) != 0):
                    dve.sem_inc(maxed, 2)
                    dve.sem_inc(neg_ok, 1)
                    for i in range(H // UH):
                        dve.wait_ge(turned, i + 1)
                        dve.tensor_copy(bias_q[:, UH * i:UH * i + UH, :],
                                        slots[:, i % 2].rearrange("p a (i x) -> p (a i) x", x=WIN)).then_inc(bias_q_ok, 1)
                    dve.wait_ge(bias_q_ok, H // UH)
                    with dve.Fori(0, B) as b:
                        with dve.Fori(0, KC) as c:
                            for h in range(HG):
                                for qb in range(KB):
                                    k = KB * h + qb
                                    n = STEPS_C * (KC * b + c) + k
                                    row = slots[:, k % 2].rearrange("p a x -> p (a x)")
                                    first = P * max(qb - 1, 0)
                                    width = P * (qb + 1) - first
                                    dve.wait_ge(scored, n + 2)
                                    if k == 0:
                                        dve.wait_ge(neg_ok, b + 1)
                                    dve.tensor_tensor(row[:, first:first + width], row[:, first:first + width],
                                                      bias_q[:, bass.ds(c * HG + h, 1), WIN - width:WIN].rearrange("p o x -> p (o x)"),
                                                      ALU.add).then_inc(added, 1)
                                    dve.wait_ge(added, n + 1)
                                    dve.tensor_reduce(most[:, bass.ds(c * STEPS_C + k, 1)], row[:, 0:P * (qb + 1)],
                                                      AX.X, ALU.max).then_inc(maxed, 1)
                        dve.wait_ge(most_ps, b + 1)
                        dve.tensor_scalar(neg[:, :], o_ps[:, 0, 0:P], -1.0, None, ALU.mult).then_inc(neg_ok, 1)
                        dve.wait_ge(neg_ok, b + 2)
                        dve.wait_ge(neg_out, 16 * GUARD * (b + 1))
                        dve.tensor_copy(neg_parts[:, 0], neg[:, :]).then_inc(split, 1)
                        dve.wait_ge(split, GUARD * b + 1)
                        dve.tensor_tensor(rest[:, :], neg[:, :], neg_parts[:, 0], ALU.subtract).then_inc(rest_ok, 1)
                        dve.wait_ge(rest_ok, b + 1)
                        dve.tensor_copy(neg_parts[:, 1], rest[:, :]).then_inc(split, 1)
                        dve.wait_ge(split, GUARD * b + 2)
                        dve.tensor_tensor(neg_parts[:, 2], rest[:, :], neg_parts[:, 1], ALU.subtract).then_inc(split, 1)

            @block.tensor
            def _(pe):
                with pe.If(pe.value_load(wide[:, :], min_val=0, max_val=1) != 0):
                    pe.sem_inc(scored, 1)
                    for i in range(H // UH):
                        if i >= 2:
                            pe.wait_ge(bias_q_ok, i - 1)
                        for h in range(UH):
                            for side in range(2):
                                col = WIN * (h % 2) + P * (1 - side)
                                ins = pe.transpose(slots[:, i % 2, h // 2, col:col + P],
                                                   bias_t[:, UH * i + h, P * side:P * side + P], ident[:, :])
                        ins.then_inc(turned, 1)
                    pe.wait_ge(bias_q_ok, H // UH)
                    with pe.Fori(0, B) as b:
                        with pe.Fori(0, KC) as c:
                            for h in range(HG):
                                if h % UH == 0:
                                    pe.wait_ge(all_ld, 16 * PARTS_DMAS * (2 * (KC * b + c) + h // UH + 1))
                                for qb in range(KB):
                                    k = KB * h + qb
                                    pe.wait_ge(maxed, STEPS_C * (KC * b + c) + k + 1)
                                    for a in range(qb // NB + 1):
                                        w = min(P * (qb + 1) - TT * a, TT)
                                        ins = pe.matmul(slots[:, k % 2, a, 0:w], q_all[:, h % UH, P * qb:P * qb + P],
                                                        k_all[:, h % UH, TT * a:TT * a + w], start=True, stop=True)
                                    ins.then_inc(scored, 1)
                        pe.wait_ge(maxed, KC * STEPS_C * (b + 1) + 2)
                        pe.wait_ge(neg_ok, b + 1)
                        pe.transpose(o_ps[:, 0, 0:P], most[:, :], ident[:, :]).then_inc(most_ps, 1)


def attend(nc, slots, o_ps, v_all, bias_t, y_t, qk_d, guard_d, k_st, q_first, st_ld, shared_at, shared_w,
           shared_raw, sw1, sw2, tile, divide, rs_row):
    with ExitStack() as ctx:
        def sb(name, shape, dt=F32):
            return ctx.enter_context(nc.sbuf_tensor(name, shape, dt))

        def sem(name):
            return ctx.enter_context(nc.semaphore(name))

        v_st = sb("v_st", [P, UNITS, KB, UH, 2 * D])
        q_st = [q_first, sb("q_second", [P, UH, T], BF16)]
        probs = sb("probs", [P, PBUFS, 2, TT])
        o_sb = overlay(nc, "o_sb", [P, UNITS, T], F32, shared_at)
        sums = sb("sums", [UH * UNITS * KB, P])
        rsums = sb("rsums", [UH * UNITS * KB, P])
        rsum_d = nc.dram_tensor("rsum_d", [UH, UNITS, T], F32, kind="Internal").ap()

        ones_ok = sem("ones_ok"); v_in = sem("v_in")
        s_ps = sem("s_ps"); biased = sem("biased"); exped = sem("exped"); pv_read = sem("pv_read"); o_ev = sem("o_ev")
        sum_in = sem("sum_in")
        rsum_ok = sem("rsum_ok"); rs_out = sem("rs_out")
        sw_ld = sem("sw_ld"); sw_high = sem("sw_high"); sw_low = sem("sw_low")

        SU = NSTEP * PAIRS
        SB = SU * UNITS
        ST_DMAS = 7
        NEAR_U = len(NEAR_STEPS) * PAIRS
        HG = H // KC
        EVAC1, EVAC0, EVAC0_FIRST, REST, INVERT = (1, 1), (4, 0), (5, 1), (3, 1), (5, 0)
        y_out, rs_in, y_norm = divide.y_out, divide.rs_in, divide.y_norm

        with nc.Block() as block:
            @block.sync
            def _(sp):
                def load_stacks(b, g):
                    buf = g % 2
                    guards = guard_d[bass.ds(b, 1)].rearrange("o g h t -> (o g) h t")
                    if g >= 2:
                        sp.wait_ge(s_ps, SB * b + SU * (g - 1))
                    elif not (isinstance(b, int) and b == 0):
                        sp.wait_ge(s_ps, SB * b - SU * (1 - g))
                    if not (isinstance(b, int) and b + g == 0):
                        load_parts(sp, qk_d, b, g, k_st[:, buf], q_st[buf], st_ld[buf])
                    sp.dma_start(q_st[buf][STACK:KROWS], guards[:, UH * g:UH * g + UH]).then_inc(st_ld[buf], 16)

                def move_unit(b, g):
                    dst = sp.snap(b * T) if not isinstance(b, int) else b * T
                    sp.wait_ge(o_ev, 2 * (UNITS * b + g + 1))
                    for j in range(UH):
                        base = D * (UH * (g % 2) + j)
                        sp.dma_start(y_t[base:base + D, g // 2, bass.ds(dst, T)], o_sb[32 * j:32 * j + D, g, :]
                                     ).then_inc(y_out[g], 16)

                def move_sums(b):
                    sp.wait_ge(o_ev, 2 * UNITS * (b + 1))
                    for j in range(UH):
                        sp.dma_start(sums[UNITS * KB * j:UNITS * KB * (j + 1), :],
                                     o_sb[32 * j + D:32 * j + D + 1].rearrange("o g (k q) -> o (g k) q", q=P)
                                     ).then_inc(sum_in, 16)

                def spread_sums(b):
                    sp.wait_ge(rsum_ok, b + 1)
                    sp.dma_start(rsum_d.rearrange("j g (k q) -> (j g k) q", q=P), rsums[:, :]).then_inc(rs_out, 16)
                    sp.wait_ge(rs_out, 16 * (b + 1))
                    sp.wait_ge(y_norm, b + 1)
                    for j in range(UH):
                        for g2 in range(2):
                            base = D * (UH * g2 + j)
                            sp.dma_start(rs_row[base:base + D], rsum_d[j, g2::2, :].partition_broadcast(D)
                                         ).then_inc(rs_in, 16)

                load_stacks(0, 0)
                load_stacks(0, 1)
                for i, src in enumerate((sw1, sw2)):
                    sp.dma_start(shared_raw[:, i].rearrange("p (k c) -> p k c", c=src.shape[1]),
                                 src.rearrange("(k p) c -> p k c", p=P)).then_inc(sw_ld, 16)
                tile.load_b1(sp)

                def body(b, before, after):
                    if before:
                        move_sums(b - 1)
                        move_unit(b - 1, UNITS - 1)
                        spread_sums(b - 1)
                    load_stacks(b, 2)
                    move_unit(b, 0)
                    load_stacks(b, 3)
                    move_unit(b, 1)
                    if after:
                        load_stacks(b + 1, 0)
                    move_unit(b, 2)
                    if after:
                        load_stacks(b + 1, 1)
                    else:
                        sp.wait_ge(v_in, UNITS * B)
                        tile.first_x(sp)
                rolled(sp, B - 1, body)
                move_sums(B - 1)
                move_unit(B - 1, UNITS - 1)
                spread_sums(B - 1)

            @block.gpsimd
            def _(pool):
                pool.sem_inc(y_norm, 1)

                def body(b, before, after):
                    if before:
                        divide.batch(pool, b - 1)
                rolled(pool, B - 1, body)
                pool.wait_ge(v_in, UNITS * B)
                pool.wait_ge(y_norm, 2)
                tile.first_high_y(pool)
                tile.residual(pool, 0)
                tile.low_y(pool, 0)

            @block.scalar
            def _(act):
                def body(b, before, after):
                    for g in range(UNITS):
                        for s in range(NSTEP):
                            w = sum(x_[3] for x_ in STEPS[s])
                            for pair in range(PAIRS):
                                k = SU * g + PAIRS * s + pair
                                if s in NEAR_STEPS:
                                    act.wait_ge(biased, NEAR_U * (UNITS * b + g) + PAIRS * NEAR_STEPS.index(s) + pair + 1)
                                else:
                                    act.wait_ge(s_ps, SB * b + k + 1)
                                if k >= PBUFS or before:
                                    act.wait_ge(pv_read, SB * b + k - PBUFS + 1)
                                nc.scalar.activation(probs[:, k % PBUFS, :, 0:w], slots[:, k % SLOTS, :, 0:w],
                                                     ACT.Exp).then_inc(exped, 1)
                rolled(act, B - 1, body)
                tile.root1(act, 0)
                act.wait_ge(sw_ld, 32)
                for g in range(UNITS):
                    act.wait_ge(y_out[g], 16 * UH * B)
                act.wait_ge(sum_in, 16 * UH * B)
                nc.scalar.activation(shared_w[0][:, 0], shared_raw[:, 0], ACT.Copy).then_inc(sw_high, 1)
                tile.high_x1(act, 0)
                nc.scalar.activation(shared_w[0][:, 1], shared_raw[:, 1], ACT.Copy).then_inc(sw_high, 1)

            @block.vector
            def _(dve):
                dve.memset(v_st[:, :, :, :, :].rearrange("p g k h d -> p (g k h) d")[:, :, D:2 * D], 1.0).then_inc(ones_ok, 1)

                def load_v(b, g):
                    src = v_all[:, bass.ds(KB * b, KB), UH * D * g:UH * D * (g + 1)]
                    dve.tensor_copy(v_st[:, g, :, :, 0:D], src.rearrange("p k (h d) -> p k h d", d=D)).then_inc(v_in, 1)

                def evacuate(b, g, half):
                    dve.wait_ge(pv_read, SB * b + SU * g + PAIRS * HALF_END[half])
                    if half == 0 and not (isinstance(b, int) and b == 0):
                        dve.wait_ge(y_out[g], 16 * UH * b)
                        dve.wait_ge(sum_in, 16 * UH * b)
                    dve.tensor_copy(o_sb[:, g, TT * half:TT * half + TT], o_ps[:, half]).then_inc(o_ev, 1)

                def invert(b):
                    dve.wait_ge(sum_in, 16 * UH * (b + 1))
                    dve.wait_ge(y_norm, b + 1)
                    dve.reciprocal(rsums[:, :], sums[:, :]).then_inc(rsum_ok, 1)

                def shared_low(i):
                    dve.wait_ge(sw_high, i + 1)
                    dve.tensor_tensor(shared_w[1][:, i], shared_raw[:, i], shared_w[0][:, i].bitcast(F32), ALU.subtract
                                      ).then_inc(sw_low, 1)

                for g in range(UNITS):
                    load_v(0, g)

                def between(b, g, s, pair, before, after):
                    if (s, pair) == EVAC1:
                        if g >= 1:
                            evacuate(b, g - 1, 1)
                        elif before:
                            evacuate(b - 1, UNITS - 1, 1)
                    if (s, pair) == (EVAC0 if g else EVAC0_FIRST):
                        evacuate(b, g, 0)
                    if (s, pair) == REST:
                        if g >= 1 and after:
                            load_v(b + 1, g - 1)
                        if g == 0 and before:
                            load_v(b, UNITS - 1)
                    if (s, pair) == INVERT and g == 0 and before:
                        invert(b - 1)

                def body(b, before, after):
                    for g in range(UNITS):
                        for s in range(NSTEP):
                            if s in NEAR_STEPS:
                                for pair in range(PAIRS):
                                    k = SU * g + PAIRS * s + pair
                                    dve.wait_ge(s_ps, SB * b + k + 1)
                                    h0 = UH * g + 2 * pair
                                    for col, w, first in near(STEPS[s]):
                                        tile = slots[:, k % SLOTS, :, col:col + w]
                                        ins = dve.tensor_tensor(tile, tile, bias_t[:, h0:h0 + 2, first:first + w], ALU.add)
                                    ins.then_inc(biased, 1)
                                    between(b, g, s, pair, before, after)
                            else:
                                for pair in range(PAIRS):
                                    between(b, g, s, pair, before, after)
                rolled(dve, B - 1, body)
                evacuate(B - 1, UNITS - 1, 1)
                tile.norm1(dve, 0)
                invert(B - 1)
                tile.norm1_end(dve, 0)
                shared_low(0)
                tile.low_x1(dve, 0)

            @block.tensor
            def _(pe):
                def scores(b, i, pair, first):
                    g, s = i // NSTEP, i % NSTEP
                    buf = g % 2
                    k = PAIRS * i + pair
                    if s == 0 and pair == 0:
                        pe.wait_ge(st_ld[buf], 16 * ST_DMAS * (2 * b + g // 2 + 1))
                    if k >= SLOTS:
                        pe.wait_ge(exped, SB * b + k - SLOTS + 1)
                    elif not first:
                        last = max(x_ for x_ in range(SB) if x_ % SLOTS == k)
                        pe.wait_ge(exped, SB * b - SB + last + 1)
                    for h in range(2):
                        j2 = 2 * pair + h
                        for half, j, q, w, col in STEPS[s]:
                            q0 = TT * half + q
                            ins = pe.matmul(slots[:, k % SLOTS, h, col:col + w],
                                            k_st[0:KROWS, buf, j2, P * j:P * j + P],
                                            q_st[buf][0:KROWS, j2, q0:q0 + w], start=True, stop=True)
                    ins.then_inc(s_ps, 1)

                def outputs(b, i, part, before):
                    g, s = i // NSTEP, i % NSTEP
                    k = PAIRS * i
                    pieces = [x for x in PIECES[s] if x[4] // (TT // 2) == part]
                    if s == 0 and part == 0:
                        pe.wait_ge(v_in, UNITS * b + g + 1)
                    if part == 0:
                        pe.wait_ge(exped, SB * b + k + PAIRS)
                    for i2, (half, j, q, w, col, first, last) in enumerate(pieces):
                        if first and (before or g):
                            pe.wait_ge(o_ev, 2 * (UNITS * b + g) + half - 1)
                        for j2 in range(UH):
                            ins = pe.matmul(o_ps[32 * j2:32 * j2 + 2 * D, half, q:q + w], v_st[:, g, j, j2, :],
                                            probs[:, (k + j2 // 2) % PBUFS, j2 % 2, col:col + w],
                                            start=first, stop=last)
                            if part and i2 == len(pieces) - 1 and j2 % 2:
                                ins.then_inc(pv_read, 1)

                pe.wait_ge(ones_ok, 1)
                for k in range(2 * PAIRS):
                    scores(0, k // PAIRS, k % PAIRS, True)

                def ahead(b, i, pair, before, after):
                    n = UNITS * NSTEP
                    if i < n:
                        scores(b, i, pair, not before)
                    elif after:
                        scores(b + 1, i - n, pair, False)

                def body(b, before, after):
                    for i in range(UNITS * NSTEP):
                        ahead(b, i + 2, 0, before, after)
                        outputs(b, i, 0, before)
                        ahead(b, i + 2, 1, before, after)
                        outputs(b, i, 1, before)
                rolled(pe, B - 1, body)
                pe.wait_ge(exped, SB * B)
                tile.project(pe, 0)
                tile.turn(pe, 0)


M = 1 + E
NQ = M * HC


class Division:
    pass


def division(nc, ctx, y_t, rs_row):
    step = Division()
    step.y_out = [ctx.enter_context(nc.semaphore(f"y_out{g}")) for g in range(UNITS)]
    step.rs_in = ctx.enter_context(nc.semaphore("rs_in"))
    step.y_norm = ctx.enter_context(nc.semaphore("y_norm"))
    RS_DMAS = 2 * UH

    def batch(pool, b):
        pool.wait_ge(step.rs_in, 16 * RS_DMAS * (b + 1))
        for g in range(UNITS):
            pool.wait_ge(step.y_out[g], 16 * UH * (b + 1))
        y = y_t[:, :, bass.ds(b * T, T)]
        pool.tensor_tensor(y, y, rs_row[:, :, :], ALU.mult).then_inc(step.y_norm, 1)

    step.batch = batch
    return step


class TileSteps:
    pass


def tile_steps(nc, ctx, slots, ident, y_t, wp_hi, wp_lo, bp_row, work_at, TILE_BYTES, x_tiles, b1_d):
    def sb(name, shape, dt=F32):
        return ctx.enter_context(nc.sbuf_tensor(name, shape, dt))

    def sem(name):
        return ctx.enter_context(nc.semaphore(name))

    x_sb, x1, x1k, base = (overlay(nc, name, [P, NB, C], F32, work_at + TILE_BYTES * i)
                           for i, name in enumerate(("x_sb", "x1", "x1k", "base")))
    yh, yl, xt_hi, xt_lo = (overlay(nc, name, [P, KC, TT], F32R, work_at + TILE_BYTES * (4 + i))
                            for i, name in enumerate(("yh", "yl", "x1t_hi", "x1t_lo")))
    x_sb, x1, x1k, base, yh, yl, xt_hi, xt_lo = (x_[:, :, :] for x_ in (x_sb, x1, x1k, base, yh, yl, xt_hi, xt_lo))
    b1_c = sb("b1_c", [P, M, HC])
    eps_c = sb("eps_c", [P, 1])
    stats = sb("stats", [P, NB, 6]); mv = sb("mv", [P, NB, 2]); sd = sb("sd", [P, NB]); rstd = sb("rstd", [P, NB])
    two_banks = slots[:, 1]

    ld_b1 = sem("ld_b1")
    x_ld2 = sem("x_ld2"); yh_ok = sem("yh_ok"); yl_ok = sem("yl_ok"); xb_ok = sem("xb_ok"); proj_ps = sem("proj_ps")
    r_ok = sem("r_ok"); st_ok = sem("st_ok"); mv_ok = sem("mv_ok"); sd_ok = sem("sd_ok"); rstd_ok = sem("rstd_ok")
    x1_ok = sem("x1_ok"); xt_ps2 = sem("xt_ps2"); xh_ok = sem("xh_ok"); xl_ok = sem("xl_ok")
    eps_ok = sem("eps_ok"); passed = sem("passed_1")
    x1k_ok = sem("x1k_ok"); l1_ps = sem("l1_ps")

    def first(t):
        return isinstance(t, int) and t == 0

    def load_b1(sp):
        for i in range(M):
            sp.dma_start(b1_c[:, i, :], b1_d[i].rearrange("(k p) -> p k", p=P),
                         allow_slow_non_contiguous=True).then_inc(ld_b1, 16)

    def first_x(sp):
        sp.dma_start(x_sb, x_tiles[:, 0]).then_inc(x_ld2, 16)

    def residual(pool, t):
        pool.wait_ge(x_ld2, 16 * (t + 1))
        pool.tensor_tensor(x_sb, x_sb, bp_row[:, :].unsqueeze(1).to_broadcast([P, NB, C]), ALU.add).then_inc(xb_ok, 1)

    def first_high_y(pool):
        pool.tensor_copy(yh, y_t[:, :, 0:TT]).then_inc(yh_ok, 1)

    def low_y(pool, t):
        pool.wait_ge(yh_ok, t + 1)
        pool.tensor_tensor(yl, y_t[:, :, token(t)], yh.bitcast(F32), ALU.subtract).then_inc(yl_ok, 1)

    def high_y(act, t):
        act.wait_ge(proj_ps, t)
        nc.scalar.activation(yh, y_t[:, :, token(t)], ACT.Copy).then_inc(yh_ok, 1)

    def root1(act, t):
        act.wait_ge(mv_ok, NB * (t + 1))
        nc.scalar.activation(sd[:, :], mv[:, :, 1], ACT.Sqrt, bias=eps_c[:, 0:1]).then_inc(sd_ok, 1)

    def high_x1(act, t):
        act.wait_ge(xt_ps2, t + 1)
        if not first(t):
            act.wait_ge(l1_ps, NQ * t)
        nc.scalar.activation(xt_hi, two_banks, ACT.Copy).then_inc(xh_ok, 1)

    def norm1(dve, t):
        if first(t):
            dve.memset(eps_c[:, :], EPS).then_inc(eps_ok, 1)
            dve.wait_ge(eps_ok, 1)
        dve.wait_ge(proj_ps, t + 1)
        dve.wait_ge(xb_ok, t + 1)
        if not first(t):
            dve.wait_ge(x1k_ok, t)
            dve.wait_ge(xt_ps2, t)
        dve.tensor_tensor(x1, two_banks.rearrange("p a (k c) -> p (a k) c", c=C), x_sb, ALU.add).then_inc(r_ok, 1)
        dve.wait_ge(r_ok, t + 1)
        for k in range(NB):
            dve.bn_stats(stats[:, k], x1[:, k]).then_inc(st_ok, 1)
        dve.wait_ge(st_ok, NB * (t + 1))
        dve.sem_inc(passed, 1)
        for k in range(NB):
            dve.bn_aggr(mv[:, k], stats[:, k]).then_inc(mv_ok, 1)

    def norm1_end(dve, t):
        dve.wait_ge(sd_ok, t + 1)
        dve.reciprocal(rstd[:, :], sd[:, :]).then_inc(rstd_ok, 1)
        dve.wait_ge(rstd_ok, t + 1)
        for k in range(NB):
            dve.tensor_scalar(x1[:, k], x1[:, k], mv[:, k, 0:1], rstd[:, k:k + 1], ALU.subtract, ALU.mult
                              ).then_inc(x1_ok, 1)

    def low_x1(dve, t):
        dve.wait_ge(xh_ok, t + 1)
        dve.tensor_tensor(xt_lo, two_banks, xt_hi.bitcast(F32), ALU.subtract).then_inc(xl_ok, 1)

    def project(pe, t):
        pe.wait_ge(yl_ok, t + 1)
        if not first(t):
            pe.wait_ge(xl_ok, t)
        for k in range(NB):
            for i, (a, w) in enumerate(PRODUCTS):
                for kc in range(KC):
                    ins = pe.matmul(slots[:, 1, k // 2, C * (k % 2):C * (k % 2) + C],
                                    (yh, yl)[a][:, kc, P * k:P * k + P], (wp_hi, wp_lo)[w][:, kc, :],
                                    start=(i == 0 and kc == 0), stop=(i == 2 and kc == KC - 1))
        ins.then_inc(proj_ps, 1)

    def turn(pe, t):
        pe.wait_ge(x1_ok, NB * (t + 1))
        for kc in range(KC):
            for k in range(NB):
                ins = pe.transpose(slots[:, 1, kc, P * k:P * k + P], x1[:, k, P * kc:P * kc + P], ident[:, :])
        ins.then_inc(xt_ps2, 1)

    steps = TileSteps()
    steps.x_sb = x_sb
    steps.x1 = x1
    steps.x1k = x1k
    steps.b1_c = b1_c
    steps.ld_b1 = ld_b1
    steps.load_b1 = load_b1
    steps.first_high_y = first_high_y
    steps.base = base
    steps.xt_hi = xt_hi
    steps.xt_lo = xt_lo
    steps.eps_c = eps_c
    steps.x_tiles = x_tiles
    steps.x_ld2 = x_ld2
    steps.r_ok = r_ok
    steps.x1_ok = x1_ok
    steps.xl_ok = xl_ok
    steps.x1k_ok = x1k_ok
    steps.l1_ps = l1_ps
    steps.first_x = first_x
    steps.residual = residual
    steps.low_y = low_y
    steps.high_y = high_y
    steps.root1 = root1
    steps.high_x1 = high_x1
    steps.norm1 = norm1
    steps.norm1_end = norm1_end
    steps.low_x1 = low_x1
    steps.project = project
    steps.turn = turn
    return steps


def feed_forward(nc, ctx, slots, o_ps, shared_w, shared_raw, out_tiles, gate_w, w1, w2, b2s, tile, divide):
    def sb(name, shape, dt=F32):
        return ctx.enter_context(nc.sbuf_tensor(name, shape, dt))

    def sem(name):
        return ctx.enter_context(nc.semaphore(name))

    x_sb, x1, x1k, base, xt_hi, xt_lo = tile.x_sb, tile.x1, tile.x1k, tile.base, tile.xt_hi, tile.xt_lo
    x_ld2, r_ok, x1_ok, xl_ok = tile.x_ld2, tile.r_ok, tile.x1_ok, tile.xl_ok
    x1k_ok, l1_ps, eps_c, b1_c = tile.x1k_ok, tile.l1_ps, tile.eps_c, tile.b1_c
    b2_d = [b2s[0]] + [b2s[1][e] for e in range(E)]

    b2_r = sb("b2_r", [P, M, C])
    gate_r = sb("gate_r", [P, E, C])
    junk = sb("junk", [P, C])
    score = sb("score", [P, E, NB]); of1 = sb("of1", [P, NB])

    half = E * 2 * KC * HID * 4
    experts_at = region(nc, ctx, "experts", 2 * half)
    experts_w = (overlay(nc, "experts_hi", [P, E, 2, KC * HID], F32R, experts_at),
                 overlay(nc, "experts_lo", [P, E, 2, KC * HID], F32R, experts_at + half))
    experts_raw = overlay(nc, "experts_raw", [P, E, 2, KC * HID], F32, experts_at + half)
    rb_hi = sb("rb_hi", [P, E, HC], F32R); rb_lo = sb("rb_lo", [P, E, HC], F32R)
    rb_f = sb("rb_f", [P, E, HC])
    base0 = sb("base0", [P, C])
    dbase = sb("dbase", [P, C])
    y2 = sb("y2", [P, NB, C]); o_out = sb("o_out", [P, NB, C])
    h_f = sb("h_f", [P, 2, TT]); h_hi = sb("h_hi", [P, 3, TT], F32R); h_lo = sb("h_lo", [P, 3, TT], F32R)
    stats2 = sb("stats2", [P, NB, 6]); mv2 = sb("mv2", [P, NB, 2]); sd2 = sb("sd2", [P, NB]); rstd2 = sb("rstd2", [P, NB])
    mask = sb("mask", [P, E, NB])

    ld_row = sem("ld_row"); score_ok = sem("score_ok"); m_ok = sem("m_ok")
    w_ld = [sem(f"w_ld{n}") for n in range(E * 4)]
    w_hi_ok = sem("w_hi_ok"); w_lo_ok = sem("w_lo_ok"); rb_ok = sem("rb_ok"); rbh_ok = sem("rbh_ok")
    rbl_ok = sem("rbl_ok"); const_ps = sem("const_ps"); const_ok = sem("const_ok"); sum_ok = sem("sum_ok")
    mask_ok = sem("mask_ok"); base_ok = sem("base_ok"); late_ok = sem("late_ok")
    passed = sem("passed_2"); w2_low = sem("w2_low")
    hf_ok = sem("hf_ok"); hh_ok = sem("hh_ok"); hl_ok = sem("hl_ok"); l2_done = sem("l2_done")
    acc_ok = sem("acc_ok"); st2_ok = sem("st2_ok"); mv2_ok = sem("mv2_ok"); sd2_ok = sem("sd2_ok")
    rstd2_ok = sem("rstd2_ok"); o_ok = sem("o_ok"); stored = sem("stored")

    l1_bank = [slots[:, 0, 0], slots[:, 0, 1]]
    acc_bank = [slots[:, 2, 0, 0:C], slots[:, 2, 1, 0:C], o_ps[:, 0, 0:C], o_ps[:, 1, 0:C]]

    def w1_of(m, part):
        return (shared_w[part][:, 0] if m == 0 else experts_w[part][:, m - 1, 0]).rearrange("p (k h) -> p k h", h=HID)

    def w2_of(m, part):
        return (shared_w[part][:, 1] if m == 0 else experts_w[part][:, m - 1, 1]).rearrange("p (k c) -> p k c", c=C)

    def piece(n, of):
        e, k = n // 4, n % 4
        return of[:, e, k // 2, HID * (k % 2):HID * (k % 2) + HID]

    LAST = TILES - 1
    LN2_AT, PROJ_AT, LN1_AT = 4, 8, 11
    CONST_AT, LATE_AT, BASE_AT = 18, 20, 22
    SPLIT_AT = 1

    def tiles(eng, body):
        rolled(eng, LAST, body)

    with nc.Block() as block:
        @block.sync
        def _(sp):
            for e in range(E):
                sp.dma_start(gate_r[:, e, :], gate_w[e].partition_broadcast(P)).then_inc(ld_row, 16)
            for i in range(M):
                sp.dma_start(b2_r[:, i, :], b2_d[i].partition_broadcast(P)).then_inc(ld_row, 16)
            for n in range(E * 4):
                e, k = n // 4, n % 4
                if k < 2:
                    src = w1[e][P * k:P * k + P, :]
                    sp.dma_start(piece(n, experts_raw), src).then_inc(w_ld[n], 16)
                else:
                    src = w2[e][TT * (k - 2):TT * (k - 2) + TT, :].rearrange("(k p) c -> p k c", p=P)
                    sp.dma_start(piece(n, experts_raw).rearrange("p (k c) -> p k c", c=C), src).then_inc(w_ld[n], 16)
            sp.sem_inc(stored, 16)

            def load_x(t):
                sp.wait_ge(r_ok, t)
                sp.dma_start(x_sb, at_tile(tile.x_tiles, t)).then_inc(x_ld2, 16)

            def store(t):
                sp.wait_ge(o_ok, NB * (t + 1))
                sp.dma_start(at_tile(out_tiles, t), o_out[:, :, :]).then_inc(stored, 16)

            def body(t, before, after):
                if after:
                    load_x(t + 1)
                if before:
                    store(t - 1)

            tiles(sp, body)
            store(LAST)
            sp.wait_ge(stored, 16 * (TILES + 1))

        @block.gpsimd
        def _(pool):
            divide.batch(pool, B - 1)
            pool.sem_inc(x1k_ok, 1)

            def prepare(t):
                tile.residual(pool, t)
                tile.low_y(pool, t)
                pool.wait_ge(x1_ok, NB * (t + 1))
                pool.wait_ge(base_ok, NB * t)
                pool.wait_ge(const_ok, 1)
                pool.tensor_tensor(x1k, x1, base0[:, :].unsqueeze(1).to_broadcast([P, NB, C]), ALU.add).then_inc(x1k_ok, 1)

            def body(t, before, after):
                if after:
                    prepare(t + 1)
            tiles(pool, body)

        @block.scalar
        def _(act):
            act.wait_ge(tile.ld_b1, 16 * M)

            def root2(t):
                act.wait_ge(mv2_ok, NB * (t + 1))
                nc.scalar.activation(sd2[:, :], mv2[:, :, 1], ACT.Sqrt, bias=eps_c[:, 0:1]).then_inc(sd2_ok, 1)

            def body(t, before, after):
                for q in range(NQ):
                    n = NQ * t + q
                    act.wait_ge(l1_ps, n + 1)
                    if q >= 2 or before:
                        act.wait_ge(hl_ok, n - 1)
                    nc.scalar.activation(h_f[:, q % 2], l1_bank[q % 2], ACT.Relu,
                                         bias=b1_c[:, q // HC, q % HC:q % HC + 1]).then_inc(hf_ok, 1)
                    act.wait_ge(hf_ok, n + 1)
                    if q >= 3 or before:
                        act.wait_ge(l2_done, n - 2)
                    nc.scalar.activation(h_hi[:, q % 3], h_f[:, q % 2], ACT.Copy).then_inc(hh_ok, 1)
                    if not before and q == 0:
                        nc.scalar.activation(rb_f[:, :, :], b1_c[:, 1:M, :], ACT.Relu).then_inc(rb_ok, 1)
                        act.wait_ge(rb_ok, 1)
                        nc.scalar.activation(rb_hi[:, :, :], rb_f[:, :, :], ACT.Copy).then_inc(rbh_ok, 1)
                    if not before and SPLIT_AT <= q < SPLIT_AT + E * 4:
                        act.wait_ge(w_ld[q - SPLIT_AT], 16)
                        nc.scalar.activation(piece(q - SPLIT_AT, experts_w[0]), piece(q - SPLIT_AT, experts_raw), ACT.Copy
                                             ).then_inc(w_hi_ok, 1)
                    if q == LN2_AT and before:
                        root2(t - 1)
                    if q == PROJ_AT - 4 and after:
                        tile.high_y(act, t + 1)
                    if q == LN1_AT + 1 and after:
                        tile.root1(act, t + 1)
                if after:
                    tile.high_x1(act, t + 1)
            tiles(act, body)
            root2(LAST)

        @block.vector
        def _(dve):
            def gate(t):
                if isinstance(t, int) and t == 0:
                    dve.wait_ge(ld_row, 16 * (M + E))
                dve.wait_ge(x1_ok, NB * (t + 1))
                for e in range(E):
                    for k in range(NB):
                        n = E * NB * t + NB * e + k
                        if not isinstance(n, int) or n:
                            dve.wait_ge(score_ok, n)
                        dve.tensor_tensor_reduce(junk[:, :], x1[:, k], gate_r[:, e], 1.0, 0.0, ALU.mult, ALU.add,
                                                 score[:, e, k:k + 1]).then_inc(score_ok, 1)
                dve.wait_ge(score_ok, E * NB * (t + 1))
                dve.tensor_tensor(of1[:, :], score[:, 1], score[:, 0], ALU.is_gt).then_inc(m_ok, 1)

            dve.tensor_tensor(shared_w[1][:, 1], shared_raw[:, 1], shared_w[0][:, 1].bitcast(F32), ALU.subtract
                              ).then_inc(w2_low, 1)

            def other_constants():
                dve.wait_ge(rbh_ok, 1)
                dve.tensor_tensor(rb_lo[:, :, :], rb_f[:, :, :], rb_hi[:, :, :].bitcast(F32), ALU.subtract).then_inc(rbl_ok, 1)
                dve.tensor_tensor(base0[:, :], b2_r[:, 0], b2_r[:, 1], ALU.add).then_inc(sum_ok, 1)
                dve.wait_ge(sum_ok, 1)
                dve.tensor_tensor(base0[:, :], base0[:, :], b2_r[:, 2], ALU.add).then_inc(sum_ok, 1)

            def constants():
                dve.wait_ge(sum_ok, 2)
                dve.wait_ge(const_ps, 1)
                dve.tensor_copy(junk[:, :], slots[:, 1, 1, 0:C]).then_inc(sum_ok, 1)
                dve.wait_ge(sum_ok, 3)
                dve.tensor_tensor(dbase[:, :], slots[:, 1, 0, 0:C], junk[:, :], ALU.subtract).then_inc(sum_ok, 1)
                dve.wait_ge(sum_ok, 4)
                dve.tensor_tensor(base0[:, :], base0[:, :], junk[:, :], ALU.add).then_inc(const_ok, 1)

            def add_late():
                dve.wait_ge(const_ok, 1)
                dve.wait_ge(acc_ok, 2 * NB)
                for k in range(NB):
                    dve.scalar_tensor_tensor(base[:, k], dbase[:, :], of1_first[:, k:k + 1], base0[:, :], ALU.mult, ALU.add
                                             ).then_inc(base_ok, 1)
                dve.wait_ge(base_ok, NB)
                dve.tensor_tensor(y2[:, :, :], y2[:, :, :], base, ALU.add).then_inc(late_ok, 1)
                dve.wait_ge(late_ok, 1)

            def add_base(t):
                dve.wait_ge(m_ok, t + 1)
                dve.wait_ge(x1k_ok, t + 1)
                for k in range(NB):
                    dve.scalar_tensor_tensor(base[:, k], dbase[:, :], of1[:, k:k + 1], x1k[:, k], ALU.mult, ALU.add
                                             ).then_inc(base_ok, 1)

            of1_first = mask[:, 1]

            def take_mask(t):
                dve.wait_ge(m_ok, t + 1)
                if not (isinstance(t, int) and t == 0):
                    dve.wait_ge(acc_ok, NB * M * t)
                dve.tensor_copy(mask[:, 1], of1[:, :]).then_inc(mask_ok, 1)
                dve.tensor_scalar(mask[:, 0], of1[:, :], -1.0, 1.0, ALU.mult, ALU.add).then_inc(mask_ok, 1)
                dve.wait_ge(mask_ok, E * (t + 1))

            def gather(t, m):
                for k in range(NB):
                    n = NB * M * t + NB * m + k
                    dve.wait_ge(l2_done, NQ * t + HC * (m + 1))
                    if m == 0:
                        start = x1 if isinstance(t, int) and t == 0 else base
                        if start is base:
                            dve.wait_ge(base_ok, NB * (t + 1))
                        dve.tensor_tensor(y2[:, k], acc_bank[k], start[:, k], ALU.add).then_inc(acc_ok, 1)
                    else:
                        dve.wait_ge(acc_ok, n - NB + 1)
                        dve.scalar_tensor_tensor(y2[:, k], acc_bank[k], mask[:, m - 1, k:k + 1], y2[:, k], ALU.mult, ALU.add
                                                 ).then_inc(acc_ok, 1)

            def norm2(t):
                dve.wait_ge(acc_ok, NB * M * (t + 1))
                for k in range(NB):
                    dve.bn_stats(stats2[:, k], y2[:, k]).then_inc(st2_ok, 1)
                dve.wait_ge(st2_ok, NB * (t + 1))
                dve.sem_inc(passed, 1)
                for k in range(NB):
                    dve.bn_aggr(mv2[:, k], stats2[:, k]).then_inc(mv2_ok, 1)

            def norm2_end(t):
                dve.wait_ge(sd2_ok, t + 1)
                dve.reciprocal(rstd2[:, :], sd2[:, :]).then_inc(rstd2_ok, 1)
                dve.wait_ge(rstd2_ok, t + 1)
                dve.wait_ge(stored, 16 * (t + 1))
                for k in range(NB):
                    dve.tensor_scalar(o_out[:, k], y2[:, k], mv2[:, k, 0:1], rstd2[:, k:k + 1], ALU.subtract, ALU.mult
                                      ).then_inc(o_ok, 1)

            def body(t, before, after):
                if before:
                    gather(t - 1, M - 1)
                if before:
                    take_mask(t)
                for q in range(NQ):
                    n = NQ * t + q
                    dve.wait_ge(hh_ok, n + 1)
                    dve.tensor_tensor(h_lo[:, q % 3], h_f[:, q % 2], h_hi[:, q % 3].bitcast(F32), ALU.subtract
                                      ).then_inc(hl_ok, 1)
                    if not before and q == 0:
                        gate(0)
                    if not before and q == 1:
                        take_mask(0)
                        other_constants()
                    if not before and SPLIT_AT <= q < SPLIT_AT + E * 4:
                        p_ = q - SPLIT_AT
                        dve.wait_ge(w_hi_ok, p_ + 1)
                        dve.tensor_tensor(piece(p_, experts_w[1]), piece(p_, experts_raw),
                                          piece(p_, experts_w[0]).bitcast(F32), ALU.subtract).then_inc(w_lo_ok, 1)
                    if before and q == LN2_AT - 2:
                        norm2(t - 1)
                    if before and q == LN2_AT + 1:
                        norm2_end(t - 1)
                    if q in (HC + 1, 2 * HC + 1):
                        gather(t, q // HC - 1)
                    if after and q == LN1_AT:
                        tile.norm1(dve, t + 1)
                    if after and q == LN1_AT + 2:
                        tile.norm1_end(dve, t + 1)
                    if after and q == LN1_AT + 3:
                        gate(t + 1)
                    if not before and q == CONST_AT + 1:
                        constants()
                    if not before and q == LATE_AT:
                        add_late()
                    if after and q == BASE_AT:
                        add_base(t + 1)
                if after:
                    tile.low_x1(dve, t + 1)
            tiles(dve, body)
            gather(LAST, M - 1)
            norm2(LAST)
            norm2_end(LAST)

        @block.tensor
        def _(pe):
            def constants():
                pe.wait_ge(rbl_ok, 1)
                pe.wait_ge(w_lo_ok, E * 4)
                pe.wait_ge(r_ok, 2)
                for e in range(E):
                    for k in range(HC):
                        for i, (a, w) in enumerate(PRODUCTS):
                            ins = pe.matmul(slots[:, 1, e, 0:C],
                                            (rb_hi, rb_lo)[a][:, e, k:k + 1].to_broadcast([P, P]),
                                            w2_of(1 + e, w)[:, k, :],
                                            start=(k == 0 and i == 0), stop=(k == HC - 1 and i == 2))
                ins.then_inc(const_ps, 1)

            def hidden(t, q, before):
                m, hc = q // HC, q % HC
                n = NQ * t + q
                if q == 0:
                    pe.wait_ge(xl_ok, t + 1)
                if m and not hc and not before:
                    pe.wait_ge(w_lo_ok, 4 * m - 2)
                if q >= 2 or before:
                    pe.wait_ge(hf_ok, n - 1)
                for i, (a, w) in enumerate(PRODUCTS):
                    for kc in range(KC):
                        ins = pe.matmul(l1_bank[q % 2], w1_of(m, w)[:, kc, P * hc:P * hc + P],
                                        (xt_hi, xt_lo)[a][:, kc, :],
                                        start=(i == 0 and kc == 0), stop=(i == 2 and kc == KC - 1))
                ins.then_inc(l1_ps, 1)

            def output(t, q, before):
                m, hc = q // HC, q % HC
                n = NQ * t + q
                pe.wait_ge(hl_ok, n + 1)
                if q == 0 and not before:
                    pe.wait_ge(w2_low, 1)
                if m and not hc and not before:
                    pe.wait_ge(w_lo_ok, 4 * m)
                for k in range(NB):
                    if hc == 0 and (m or before):
                        pe.wait_ge(acc_ok, NB * M * t + NB * (m - 1) + k + 1)
                    for i, (a, w) in enumerate(PRODUCTS):
                        ins = pe.matmul(acc_bank[k], (h_hi, h_lo)[a][:, q % 3, P * k:P * k + P],
                                        w2_of(m, w)[:, hc, :],
                                        start=(hc == 0 and i == 0), stop=(hc == HC - 1 and i == 2))
                ins.then_inc(l2_done, 1)

            def body(t, before, after):
                hidden(t, 0, before)
                hidden(t, 1, before)
                for q in range(NQ):
                    if q + 2 < NQ:
                        hidden(t, q + 2, before)
                    if after and q == PROJ_AT:
                        tile.project(pe, t + 1)
                    if not before and q == CONST_AT:
                        constants()
                    if after and q == NQ - 2:
                        if not before:
                            pe.wait_ge(const_ok, 1)
                        tile.turn(pe, t + 1)
                    output(t, q, before)
            tiles(pe, body)


def token(t):
    return bass.ds(t * TT, TT)


def at_tile(dram, t):
    return dram[:, bass.ds(t, 1)].rearrange("p n k c -> p (n k) c")


_INS = ['L0_attn_x', 'L0_attn_W_attn', 'L0_attn_b_attn', 'L0_attn_W_proj', 'L0_attn_b_proj', 'L0_attn_rel_emb',
        'L0_ffn_gate_w', 'L0_ffn_w1', 'L0_ffn_b1', 'L0_ffn_w2', 'L0_ffn_b2', 'L0_ffn_sw1', 'L0_ffn_sb1',
        'L0_ffn_sw2', 'L0_ffn_sb2']


def kernel(**inputs):
    from concourse import bacc
    from concourse.bass_utils import run_bass_kernel_spmd

    nc = bacc.Bacc("TRN2", target_bir_lowering=False, num_devices=1)
    arrays, args = {}, []
    for name in _INS:
        arrays[name] = np.ascontiguousarray(inputs[name])
        args.append(nc.dram_tensor(name, arrays[name].shape, F32, kind="ExternalInput").ap())
    arrays["buckets"] = bucket_rows()
    args.append(nc.dram_tensor("buckets", arrays["buckets"].shape, F32, kind="ExternalInput").ap())
    args.append(nc.dram_tensor("out", (B, T, C), F32, kind="ExternalOutput").ap())
    build(nc, *args)
    return run_bass_kernel_spmd(nc, [arrays], core_ids=[0]).results[0]["out"]
```
